# Optimizing a Trainium2 kernel written in Bass

```python
import numpy as np
import jax
import jax.numpy as jnp

def _softmax(x, axis=-1):
    return jax.nn.softmax(x, axis=axis)

def _gelu(x):
    return jax.nn.gelu(x, approximate=True)

def _silu(x):
    return jax.nn.silu(x)

def _sigmoid(x):
    return jax.nn.sigmoid(x)

def _layernorm(x, axis=-1, eps=1e-05):
    m = jnp.mean(x, axis=axis, keepdims=True)
    v = jnp.var(x, axis=axis, keepdims=True)
    return (x - m) / jnp.sqrt(v + eps)

def _scatter_add(tgt, idx, src, axis=0):
    return tgt.at[idx].add(src)

def _segment_sum(src, seg, n):
    return jax.ops.segment_sum(src, seg, n)
kernel_name = 'mk_decoder_postln_d1_seqx_r8_0f0d08'

def setup_inputs(seed: int=0):
    np.random.seed(seed)
    _w = jnp.asarray

    def _rec_inputs():
        import jax
        import jax.numpy as jnp
        _rk = jax.random.key(seed)
        x = 7.22e-05 + 1 * jax.random.normal(jax.random.fold_in(_rk, 1), (4, 256, 256), jnp.float32)
        _lenS = 256 - jax.random.randint(jax.random.fold_in(_rk, 7), (4,), 0, max(1, 256 // 4) + 1, jnp.int32)
        _lenS2 = 256 - jax.random.randint(jax.random.fold_in(_rk, 8), (4,), 0, max(1, 256 // 4) + 1, jnp.int32)
        _ctx_1024P = jax.random.normal(jax.random.fold_in(_rk, 11), (4, 16, 128), jnp.float32)
        _ctx_1024c = jax.random.dirichlet(jax.random.fold_in(_rk, 511), 0.3 * jnp.ones((16,), jnp.float32), (4, 256))
        _ctx_1024t = jnp.einsum('bsk,bkd->bsd', _ctx_1024c, _ctx_1024P)
        _ctx_1024t = _ctx_1024t * jax.lax.rsqrt(jnp.mean(jnp.square(_ctx_1024t)) + 1e-12) * 0.953939
        ctx_1024 = 2.81802e-05 + 1.00001 * (_ctx_1024t + 0.3 * jax.random.normal(jax.random.fold_in(_rk, 611), (4, 256, 128), jnp.float32))
        return (x, ctx_1024)
    x, ctx_1024 = _rec_inputs()

    def _L0_attn_setup():
        import jax, jax.numpy as jnp
        import numpy as np
        B, T, C, H = (2, 256, 256, 16)
        D = C // H
        EPS = 1e-05

        def _wkv_scan(r, k, v, w, u):
            rT = jnp.moveaxis(r, 1, 0)
            kT = jnp.moveaxis(k, 1, 0)
            vT = jnp.moveaxis(v, 1, 0)

            def step(S, inp):
                r_t, k_t, v_t = inp
                kv = k_t[..., :, None] * v_t[..., None, :]
                o = jnp.einsum('bhi,bhij->bhj', r_t, S + u[None, :, :, None] * kv)
                S = w[None, :, :, None] * S + kv
                return (S, o)
            S0 = jnp.zeros((r.shape[0], H, D, D), r.dtype)
            _, o = jax.lax.scan(step, S0, (rT, kT, vT))
            return jnp.moveaxis(o, 0, 1)
        key = jax.random.key(seed)
        ks = jax.random.split(key, 12)
        return {'x': jax.random.normal(ks[0], (B, T, C), jnp.float32), 'Wr': jax.random.normal(ks[1], (C, C), jnp.float32) * (1.0 / np.sqrt(C)), 'Wk': jax.random.normal(ks[2], (C, C), jnp.float32) * (1.0 / np.sqrt(C)), 'Wv': jax.random.normal(ks[3], (C, C), jnp.float32) * (1.0 / np.sqrt(C)), 'Wg': jax.random.normal(ks[4], (C, C), jnp.float32) * (1.0 / np.sqrt(C)), 'Wo': jax.random.normal(ks[5], (C, C), jnp.float32) * (1.0 / np.sqrt(C)), 'time_decay': jax.random.normal(ks[6], (H, D), jnp.float32), 'time_first': jax.random.normal(ks[7], (H, D), jnp.float32) * 0.1, 'tm_k': jax.random.uniform(ks[8], (C,), jnp.float32, -0.1, 0.1) + 1.0, 'tm_v': jax.random.uniform(ks[9], (C,), jnp.float32, -0.1, 0.1) + 1.0, 'tm_r': jax.random.uniform(ks[10], (C,), jnp.float32, -0.1, 0.1) + 1.0, 'tm_g': jax.random.uniform(ks[11], (C,), jnp.float32, -0.1, 0.1) + 1.0, 'ln_w': jnp.ones((C,), jnp.float32), 'ln_b': jnp.zeros((C,), jnp.float32)}
    _L0_attn_all = _L0_attn_setup()
    _L0_attn_in = {k: v for k, v in _L0_attn_all.items() if k in ('Wr', 'Wk', 'Wv', 'Wg', 'Wo', 'time_decay', 'time_first', 'tm_k', 'tm_v', 'tm_r', 'tm_g', 'ln_w', 'ln_b')}
    del _L0_attn_all

    def _L0_xattn_setup():
        import jax, jax.numpy as jnp
        import numpy as np
        key = jax.random.key(seed)
        ks = jax.random.split(key, 6)
        B, L, N, C, D = (8, 64, 256, 128, 128)
        return {'teacher_logits': jax.random.normal(ks[0], (B, L, N), dtype=jnp.float32), 'teacher_features': jax.random.normal(ks[1], (B, N, C), dtype=jnp.float32), 'Wq': jax.random.normal(ks[2], (D, C), dtype=jnp.float32) * (1.0 / np.sqrt(C)), 'bq': jnp.zeros((D,), dtype=jnp.float32), 'Wk': jax.random.normal(ks[3], (D, C), dtype=jnp.float32) * (1.0 / np.sqrt(C)), 'bk': jnp.zeros((D,), dtype=jnp.float32)}
    _L0_xattn_all = _L0_xattn_setup()
    _L0_xattn_in = {k: v for k, v in _L0_xattn_all.items() if k in ('Wq', 'bq', 'Wk', 'bk')}
    del _L0_xattn_all

    def _L0_ffn_setup():
        import jax, jax.numpy as jnp
        import numpy as np
        BLOCK_SIZE = 32
        HIDDEN_SIZE = 256
        MLP_DIM = 2048
        NVFP4_LUT = jnp.array([0.0, 0.5, 1.0, 1.5, 2.0, 3.0, 4.0, 6.0, 0.0, -0.5, -1.0, -1.5, -2.0, -3.0, -4.0, -6.0], dtype=jnp.float32)

        def dequant_nvfp4(W_packed, scales, block=BLOCK_SIZE):
            N = W_packed.shape[0]
            low = W_packed & 15
            high = W_packed >> 4 & 15
            idx = jnp.stack([low, high], axis=-1).reshape(N, -1)
            vals = NVFP4_LUT[idx]
            K = vals.shape[1]
            vals = vals.reshape(N, K // block, block) * scales[:, :, None]
            return vals.reshape(N, K)
        key = jax.random.key(seed)
        ks = jax.random.split(key, 7)
        x = jax.random.normal(ks[0], (4, 32, HIDDEN_SIZE), dtype=jnp.float32)
        gate_W_packed = jax.random.randint(ks[1], (MLP_DIM, HIDDEN_SIZE // 2), 0, 32, dtype=jnp.int32)
        gate_scales = jax.random.uniform(ks[2], (MLP_DIM, HIDDEN_SIZE // BLOCK_SIZE), dtype=jnp.float32) * 0.1 + 0.001
        up_W_packed = jax.random.randint(ks[3], (MLP_DIM, HIDDEN_SIZE // 2), 0, 32, dtype=jnp.int32)
        up_scales = jax.random.uniform(ks[4], (MLP_DIM, HIDDEN_SIZE // BLOCK_SIZE), dtype=jnp.float32) * 0.1 + 0.001
        down_W_packed = jax.random.randint(ks[5], (HIDDEN_SIZE, MLP_DIM // 2), 0, 32, dtype=jnp.int32)
        down_scales = jax.random.uniform(ks[6], (HIDDEN_SIZE, MLP_DIM // BLOCK_SIZE), dtype=jnp.float32) * 0.1 + 0.001
        return {'x': x, 'gate_W_packed': gate_W_packed, 'gate_scales': gate_scales, 'up_W_packed': up_W_packed, 'up_scales': up_scales, 'down_W_packed': down_W_packed, 'down_scales': down_scales}
    _L0_ffn_all = _L0_ffn_setup()
    _L0_ffn_in = {k: v for k, v in _L0_ffn_all.items() if k in ('gate_W_packed', 'gate_scales', 'up_W_packed', 'up_scales', 'down_W_packed', 'down_scales')}
    del _L0_ffn_all
    return {'x': x, 'ctx_1024': ctx_1024, 'L0_attn_Wr': _L0_attn_in['Wr'], 'L0_attn_Wk': _L0_attn_in['Wk'], 'L0_attn_Wv': _L0_attn_in['Wv'], 'L0_attn_Wg': _L0_attn_in['Wg'], 'L0_attn_Wo': _L0_attn_in['Wo'], 'L0_attn_time_decay': _L0_attn_in['time_decay'], 'L0_attn_time_first': _L0_attn_in['time_first'], 'L0_attn_tm_k': _L0_attn_in['tm_k'], 'L0_attn_tm_v': _L0_attn_in['tm_v'], 'L0_attn_tm_r': _L0_attn_in['tm_r'], 'L0_attn_tm_g': _L0_attn_in['tm_g'], 'L0_attn_ln_w': _L0_attn_in['ln_w'], 'L0_attn_ln_b': _L0_attn_in['ln_b'], 'L0_xattn_Wq': _L0_xattn_in['Wq'], 'L0_xattn_bq': _L0_xattn_in['bq'], 'L0_xattn_Wk': _L0_xattn_in['Wk'], 'L0_xattn_bk': _L0_xattn_in['bk'], 'L0_ffn_gate_W_packed': _L0_ffn_in['gate_W_packed'], 'L0_ffn_gate_scales': _L0_ffn_in['gate_scales'], 'L0_ffn_up_W_packed': _L0_ffn_in['up_W_packed'], 'L0_ffn_up_scales': _L0_ffn_in['up_scales'], 'L0_ffn_down_W_packed': _L0_ffn_in['down_W_packed'], 'L0_ffn_down_scales': _L0_ffn_in['down_scales']}

def reference(x, ctx_1024, L0_attn_Wr, L0_attn_Wk, L0_attn_Wv, L0_attn_Wg, L0_attn_Wo, L0_attn_time_decay, L0_attn_time_first, L0_attn_tm_k, L0_attn_tm_v, L0_attn_tm_r, L0_attn_tm_g, L0_attn_ln_w, L0_attn_ln_b, L0_xattn_Wq, L0_xattn_bq, L0_xattn_Wk, L0_xattn_bk, L0_ffn_gate_W_packed, L0_ffn_gate_scales, L0_ffn_up_W_packed, L0_ffn_up_scales, L0_ffn_down_W_packed, L0_ffn_down_scales):
    import jax
    import jax.numpy as jnp

    def _L0_attn_ref(x, Wr, Wk, Wv, Wg, Wo, time_decay, time_first, tm_k, tm_v, tm_r, tm_g, ln_w, ln_b):
        import jax, jax.numpy as jnp
        import numpy as np
        B, T, C, H = (2, 256, 256, 16)
        D = C // H
        EPS = 1e-05

        def _wkv_scan(r, k, v, w, u):
            rT = jnp.moveaxis(r, 1, 0)
            kT = jnp.moveaxis(k, 1, 0)
            vT = jnp.moveaxis(v, 1, 0)

            def step(S, inp):
                r_t, k_t, v_t = inp
                kv = k_t[..., :, None] * v_t[..., None, :]
                o = jnp.einsum('bhi,bhij->bhj', r_t, S + u[None, :, :, None] * kv)
                S = w[None, :, :, None] * S + kv
                return (S, o)
            S0 = jnp.zeros((r.shape[0], H, D, D), r.dtype)
            _, o = jax.lax.scan(step, S0, (rT, kT, vT))
            return jnp.moveaxis(o, 0, 1)
        Bx, Tx, Cx = x.shape
        xx = jnp.concatenate([x[:, 1:2, :], x[:, :-1, :]], axis=1) - x
        xk = x + xx * tm_k
        xv = x + xx * tm_v
        xr = x + xx * tm_r
        xg = x + xx * tm_g
        r = xr @ Wr.T
        k = xk @ Wk.T
        v = xv @ Wv.T
        g = jax.nn.sigmoid(xg @ Wg.T)
        w = jnp.exp(-jnp.exp(time_decay))
        r = r.reshape(Bx, Tx, H, D)
        k = k.reshape(Bx, Tx, H, D)
        v = v.reshape(Bx, Tx, H, D)
        o = _wkv_scan(r, k, v, w, time_first)
        o = o.reshape(Bx, Tx, Cx)
        y = o * g @ Wo.T
        mu = jnp.mean(y, axis=-1, keepdims=True)
        var = jnp.mean((y - mu) ** 2, axis=-1, keepdims=True)
        return (y - mu) * jax.lax.rsqrt(var + EPS) * ln_w + ln_b

    def _L0_xattn_ref(teacher_logits, teacher_features, Wq, bq, Wk, bk):
        import jax, jax.numpy as jnp
        import numpy as np
        query = jnp.einsum('bnc,dc->bnd', teacher_features, Wq) + bq
        key = jnp.einsum('bnc,dc->bnd', teacher_features, Wk) + bk
        energy = jnp.einsum('bnd,bmd->bnm', query, key)
        attention = jax.nn.softmax(energy, axis=-1)
        x_m = jnp.einsum('bln,bmn->blm', teacher_logits, attention)
        return x_m

    def _L0_ffn_ref(x, gate_W_packed, gate_scales, up_W_packed, up_scales, down_W_packed, down_scales):
        import jax, jax.numpy as jnp
        import numpy as np
        BLOCK_SIZE = 32
        HIDDEN_SIZE = 256
        MLP_DIM = 2048
        NVFP4_LUT = jnp.array([0.0, 0.5, 1.0, 1.5, 2.0, 3.0, 4.0, 6.0, 0.0, -0.5, -1.0, -1.5, -2.0, -3.0, -4.0, -6.0], dtype=jnp.float32)

        def dequant_nvfp4(W_packed, scales, block=BLOCK_SIZE):
            N = W_packed.shape[0]
            low = W_packed & 15
            high = W_packed >> 4 & 15
            idx = jnp.stack([low, high], axis=-1).reshape(N, -1)
            vals = NVFP4_LUT[idx]
            K = vals.shape[1]
            vals = vals.reshape(N, K // block, block) * scales[:, :, None]
            return vals.reshape(N, K)
        B, S, H = x.shape
        xt = x.reshape(B * S, H)
        Wg = dequant_nvfp4(gate_W_packed, gate_scales)
        Wu = dequant_nvfp4(up_W_packed, up_scales)
        Wd = dequant_nvfp4(down_W_packed, down_scales)
        gate = jnp.einsum('th,nh->tn', xt, Wg)
        up = jnp.einsum('th,nh->tn', xt, Wu)
        gelu = jnp.tanh(0.7978845608028654 * (gate + 0.044715 * gate ** 3)) * gate * 0.5 + gate * 0.5
        inter = gelu * up
        out = jnp.einsum('tn,hn->th', inter, Wd)
        return out.reshape(B, S, H)
    x = _layernorm(x + _L0_attn_ref(x, L0_attn_Wr, L0_attn_Wk, L0_attn_Wv, L0_attn_Wg, L0_attn_Wo, L0_attn_time_decay, L0_attn_time_first, L0_attn_tm_k, L0_attn_tm_v, L0_attn_tm_r, L0_attn_tm_g, L0_attn_ln_w, L0_attn_ln_b), axis=-1)
    x = _layernorm(x + _L0_xattn_ref(x, ctx_1024, L0_xattn_Wq, L0_xattn_bq, L0_xattn_Wk, L0_xattn_bk), axis=-1)
    x = _layernorm(x + _L0_ffn_ref(x, L0_ffn_gate_W_packed, L0_ffn_gate_scales, L0_ffn_up_W_packed, L0_ffn_up_scales, L0_ffn_down_W_packed, L0_ffn_down_scales), axis=-1)
    return x

_drawn_inputs = setup_inputs


def setup_inputs(seed=0):
    import zlib

    import numpy as np

    out = dict(_drawn_inputs(seed))
    spreads = {'L0_attn_ln_w': (1.0, 0.2),
     'L0_attn_ln_b': (0.0, 0.1),
     'L0_xattn_bq': (0.0, 0.1),
     'L0_xattn_bk': (0.0, 0.1)}
    factors = {}
    for name, (base, spread) in spreads.items():
        noise = np.random.default_rng([zlib.crc32(name.encode()), seed]).standard_normal(out[name].shape)
        drawn = base * np.exp(spread * noise) if base else spread * noise
        out[name] = jnp.asarray(drawn.astype(out[name].dtype))
    for name, factor in factors.items():
        out[name] = (out[name] * factor).astype(out[name].dtype)
    return out
```

```python
from contextlib import ExitStack

import concourse.bass as bass
from concourse import mybir

ALU = mybir.AluOpType
ACT = mybir.ActivationFunctionType
F32 = mybir.dt.float32
F16 = mybir.dt.float16
I32 = mybir.dt.int32
U16 = mybir.dt.uint16
AX = mybir.AxisListType
RMAX = bass.bass_isa.ReduceOp.max

P = 128
B, T, C = 4, 256, 256
N = B * T
D = 16
HALVES = C // P
TILES = N // P
TB = 512
GROUPS = N // TB
GT = TB // P
MLP = 2048
NT = MLP // P
EPS = 1e-5
X_UP = 2048.0
W_UP = 4096.0
I_DOWN = 2.0 ** -8
CODE_UP = 2.0 ** 14


def decoder_layer(nc, x_chan, x_tok, ctx_chan, w_chan, chan_vecs, ln_vecs, xq_chan, xq_bias,
                  packed, scale_rows_in, scale_rows_out, scale_flat, consts, out):
    with ExitStack() as stack:
        def sb(name, shape, dt=F32):
            return stack.enter_context(nc.sbuf_tensor(name, shape, dt))

        def sem(name):
            return stack.enter_context(nc.semaphore(name))

        region_a = sb("region_a", [P, 8192])
        xT = region_a[:, 0:2048].rearrange("p (h t) -> p h t", h=2)
        xx = region_a[:, 2048:4096].rearrange("p (h t) -> p h t", h=2)
        mix = region_a[:, 4096:8192].rearrange("p (m h t) -> p m h t", m=2, h=2)
        diag = region_a[:, 0:1024]
        bits = region_a[:, 1024:2048].bitcast(U16).rearrange("p (s n) -> p s n", s=2)
        og = region_a[:, 2048:4096].rearrange("p (h t) -> p h t", h=2)
        full = region_a[:, 4096:6144].rearrange("p (s n) -> p s n", s=2)
        xtok = region_a[:, 6144:8192].rearrange("p (n c) -> p n c", n=TILES)
        inter1 = region_a[:, :].bitcast(F16).rearrange("p (m n t) -> p m n t", m=2, n=NT)

        region_b = sb("region_b", [P, 8192])
        vkrg = region_b[:, :].rearrange("p (m h t) -> p m h t", m=4, h=2)
        inter0 = region_b[:, :].bitcast(F16).rearrange("p (m n t) -> p m n t", m=2, n=NT)
        inter = [inter0, inter1]

        region_c = sb("region_c", [P, 8192])
        packed_sb = region_c[:, 0:6144].bitcast(I32).rearrange("p (w n) -> p w n", w=3)
        kv = region_c[:, 0:2048].rearrange("p (s t) -> p s t", s=2)
        state = region_c[:, 2048:5120].rearrange("p (s t) -> p s t", s=3)
        prod = region_c[:, 5120:8192].rearrange("p (s t) -> p s t", s=3)
        x1 = region_c[:, 0:2048].rearrange("p (n c) -> p n c", n=TILES)
        x1T = region_c[:, 2048:4096].rearrange("p (g k t) -> p g k t", g=GROUPS, k=2)
        x2 = region_c[:, 4096:6144].rearrange("p (n c) -> p n c", n=TILES)
        ztmp = region_c[:, 6144:8192].rearrange("p (n c) -> p n c", n=TILES)

        wo = sb("wo", [P, 2, C])
        w16 = sb("w16", [P, 3, 2, 2, 2048], F16)
        wproj = w16[:, 1].rearrange("p e m n -> p (e m n)").bitcast(F32).rearrange(
            "p (m k n) -> p m k n", m=8, k=2)[:, 0:4]
        early = w16[:, 2].rearrange("p e m n -> p (e m n)").bitcast(F32)
        ctxT = early[:, 0:1024]
        queryT = early[:, 1024:2048]
        keyT = early[:, 2048:3072]
        wqk = early[:, 3072:3328].rearrange("p (m n) -> p m n", m=2)
        att = w16[:, 0].rearrange("p e m n -> p (e m n)").bitcast(F32)[:, 0:2048].rearrange(
            "p (n k) -> p n k", n=TILES)
        p16 = sb("p16", [P, 3, 2048], U16)
        scales = sb("scales", [P, 3, 2048])
        x2T16 = scales[:, 0, :].bitcast(F16).rearrange("p (m k t) -> p m k t", m=2, k=2)
        gelu = scales[:, 1, 0:1024].rearrange("p (s t) -> p s t", s=2)
        inter32 = scales[:, 1, 1024:2048].rearrange("p (s t) -> p s t", s=2)
        ff = scales[:, 2, :].rearrange("p (n c) -> p n c", n=TILES)
        attT = sb("attT", [P, 2, TILES, P])
        const = sb("const", [P, 648])
        ident = const[:, 0:128]
        head_sum = const[:, 128:256]
        head_pick = const[:, 256:504]
        head_spread = const[:, 504:632]
        lane = const[:, 632:648]
        bcast = sb("bcast", [P, D, P])
        keep = sb("keep", [P, TB])
        ln = sb("ln", [P, 2, C])
        cvec = sb("cvec", [P, 2, 6])
        decay = sb("decay", [P, 2, 2])
        qkb = sb("qkb", [P, 2])
        flat = sb("flat", [P, 3, P])
        gm = sb("gm", [P, 8, 3])
        smax = sb("smax", [P, 4, TILES])
        lnst = sb("lnst", [P, 2, 6])
        mv = sb("mv", [P, 4, TILES, 2])
        rstd = sb("rstd", [P, 4, TILES])
        eps = sb("eps", [P, 1])

        psA = [stack.enter_context(nc.psum_tensor(f"psA{i}", [P, 1024], F32)) for i in range(2)]
        psO = stack.enter_context(nc.psum_tensor("psO", [P, 1024], F32))
        psW = stack.enter_context(nc.psum_tensor("psW", [P, TB], F32))
        psM = stack.enter_context(nc.psum_tensor("psM", [P, TB], F32))
        gate_ps = [psO[:, 0:TB], psW[:, :]]
        up_ps = [psO[:, TB:1024], psM[:, :]]

        loads = ["const", "xT", "cvec", "wproj", "ctxT", "wqk", "qkb", "packed", "flat", "scales",
                 "wo", "ln", "xtok"]
        loaded = {n: sem("loaded_" + n) for n in loads}
        vec = sem("vec_steps")
        mix_ready = sem("mix_ready")
        p16_ready = sem("p16_ready")
        proj_done = sem("proj_done")
        proj_copied = sem("proj_copied")
        decay_ready = sem("decay_ready")
        act_steps = sem("act_steps")
        gpool = sem("gpool")
        allmax = sem("allmax")
        absmax = sem("absmax")
        gready = sem("gready")
        scale_ready = sem("scale_ready")
        bcast_ready = sem("bcast_ready")
        qk_ps = sem("qk_ps")
        qk_copied = sem("qk_copied")
        energy_done = sem("energy_done")
        negmax_ready = sem("negmax_ready")
        exp_done = sem("exp_done")
        att_ready = sem("att_ready")
        attT_ps = sem("attT_ps")
        attT_copied = sem("attT_copied")
        spread_done = sem("spread_done")
        spread_used = sem("spread_used")
        decay_set = sem("decay_set")
        state_ready = sem("state_ready")
        prod_ready = sem("prod_ready")
        sum_done = sem("sum_done")
        half_read = sem("half_read")
        og_ready = sem("og_ready")
        full_ready = sem("full_ready")
        bits_ready = sem("bits_ready")
        hi_ready = sem("hi_ready")
        lo_ready = sem("lo_ready")
        y_done = sem("y_done")
        var_ready = sem("var_ready")
        sqrt_done = sem("sqrt_done")
        x1_ready = sem("x1_ready")
        z_ready = sem("z_ready")
        zw_ready = sem("zw_ready")
        x1T_ps = sem("x1T_ps")
        x1T_copied = sem("x1T_copied")
        xm_done = sem("xm_done")
        x2_ready = sem("x2_ready")
        x2T_ps = sem("x2T_ps")
        x2hi_ready = sem("x2hi_ready")
        x2lo_ready = sem("x2lo_ready")
        gate_done = sem("gate_done")
        up_done = sem("up_done")
        gelu_done = sem("gelu_done")
        inter_ready = sem("inter_ready")
        ihi_ready = sem("ihi_ready")
        ilo_ready = sem("ilo_ready")
        down_done = sem("down_done")
        ff_ready = sem("ff_ready")
        stored = sem("stored")

        PIECES = [(w, e, f) for w in range(3) for e in range(2) for f in range(2)]
        NP = len(PIECES)
        STEPS = [(h, j) for h in range(HALVES) for j in [None] + list(range(D))]
        SCANS = [(h, j) for h in range(HALVES) for j in range(D)]

        def piece_at(step):
            return (step - 2) // 2 if step >= 2 and step % 2 == 0 and (step - 2) // 2 < NP else None

        PLAN = [("y", 0), ("x1T", 0), ("xm", 0), ("x2T", 0), ("y", 1)]
        PLAN += [("ffn", 0, 0), ("ffn", 0, 1), ("x1T", 1), ("ffn", 0, 2), ("ffn", 0, 3), ("ffn", 0, 4), ("xm", 1),
                 ("ffn", 0, 5), ("ffn", 0, 6), ("ffn", 0, 7), ("ffn", 0, 8), ("x2T", 1)]
        PLAN += [("ffn", 0, n) for n in range(9, NT)] + [("ffn", 1, 0), ("ffn", 1, 1), ("down", 0)]
        PLAN += [("ffn", 1, n) for n in range(2, NT)] + [("down", 1)]

        block = stack.enter_context(nc.Block())

        @block.sync
        def _(sp):
            sp.dma_start(xT, x_chan.rearrange("(h p) t -> p h t", p=P)).then_inc(loaded["xT"], 16)
            sp.dma_start(cvec[:, :, :], chan_vecs.rearrange("(h p) v -> p h v", p=P)).then_inc(loaded["cvec"], 16)
            sp.dma_start(wproj, w_chan[0:4].rearrange("m (k p) n -> p m k n", p=P)).then_inc(loaded["wproj"], 16)
            sp.dma_start(const[:, :], consts).then_inc(loaded["const"], 16)
            sp.dma_start(ctxT, ctx_chan).then_inc(loaded["ctxT"], 16)
            sp.dma_start(wqk, xq_chan.rearrange("m p n -> p m n")).then_inc(loaded["wqk"], 16)
            sp.dma_start(qkb[:, :], xq_bias).then_inc(loaded["qkb"], 16)
            sp.dma_start(wo[:, :, :], w_chan[4].rearrange("(k p) n -> p k n", p=P)).then_inc(loaded["wo"], 16)
            sp.dma_start(ln[:, :, :], ln_vecs.partition_broadcast(P)).then_inc(loaded["ln"], 16)
            sp.wait_ge(proj_done, 8)
            sp.dma_start(xtok, x_tok.rearrange("(n p) c -> p n c", p=P)).then_inc(loaded["xtok"], 16)
            for g in range(GROUPS):
                sp.wait_ge(ff_ready, g + 1)
                sp.dma_start(out[g * TB:(g + 1) * TB].rearrange("(n p) c -> p n c", p=P),
                             ztmp[:, GT * g:GT * g + GT, :]).then_inc(stored, 16)
            sp.wait_ge(stored, 16 * GROUPS)

        @block.scalar
        def _(act):
            act.dma_start(flat[:, :, :], scale_flat.rearrange("w (p n) -> p w n", p=P)).then_inc(loaded["flat"], 16)
            act.dma_start(packed_sb, packed.rearrange("w p n -> p w n")).then_inc(loaded["packed"], 16)
            for w in range(2):
                for k in range(8):
                    act.dma_start(scales[16 * k:16 * k + 16, w, :],
                                  scale_rows_in[w, k:k + 1, :].broadcast_to([16, 2048])).then_inc(loaded["scales"], 16)
            for k in range(8):
                act.dma_start(scales[16 * k:16 * k + 16, 2, :].rearrange("p (c n) -> p c n", c=8),
                              scale_rows_out[:, k, :].partition_broadcast(16)).then_inc(loaded["scales"], 16)
            act.wait_ge(loaded["cvec"], 16)
            act.activation(decay[:, :, 0], cvec[:, :, 4], ACT.Exp).then_inc(act_steps, 1)
            act.wait_ge(act_steps, 1)
            act.activation(decay[:, :, 1], decay[:, :, 0], ACT.Exp, scale=-1.0).then_inc(decay_ready, 1)
            for q in range(8):
                act.wait_ge(proj_done, q + 1)
                act.activation(vkrg[:, q // 2, q % 2, :], psA[q % 2][:, :],
                               ACT.Sigmoid if q >= 6 else ACT.Copy).then_inc(proj_copied, 1)
            act.wait_ge(loaded["qkb"], 16)
            for m, dst in enumerate((queryT, keyT)):
                act.wait_ge(qk_ps, m + 1)
                act.activation(dst, psA[m][:, :], ACT.Identity, bias=qkb[:, m:m + 1]).then_inc(qk_copied, 1)
            act.wait_ge(negmax_ready, 1)
            for n in range(TILES):
                act.activation(att[:, n, :], psA[n // 4][:, (n % 4) * 256:(n % 4) * 256 + 256], ACT.Exp,
                               bias=smax[:, 0, n:n + 1], accum_out=smax[:, 1, n:n + 1]).then_inc(exp_done, 1)
            for i in range(2):
                act.wait_ge(attT_ps, i + 1)
                act.activation(attT[:, :, 4 * i:4 * i + 4, :],
                               psA[i][:, :].rearrange("p (n k q) -> p k n q", n=4, k=2), ACT.Copy)\
                   .then_inc(attT_copied, 1)
            act.wait_ge(gready, 1)
            act.wait_ge(loaded["scales"], 16 * 24)
            for w in range(3):
                act.activation(scales[:, w, :], scales[:, w, :], ACT.Copy, scale=gm[:, 3, w:w + 1])\
                   .then_inc(scale_ready, 1)
            for d, (w, e, f) in enumerate(PIECES):
                act.wait_ge(full_ready, d + 1)
                act.activation(w16[:, w, e, 0, 1024 * f:1024 * f + 1024], full[:, d % 2, :], ACT.Copy)\
                   .then_inc(hi_ready, 1)

            n_sqrt = 0
            for item in PLAN:
                if item[0] == "y":
                    g = item[1]
                    for i in range(2):
                        n_sqrt += 1
                        act.wait_ge(var_ready, n_sqrt)
                        act.activation(rstd[:, i, GT * g:GT * g + GT], mv[:, i, GT * g:GT * g + GT, 1], ACT.Sqrt,
                                       bias=eps[:, 0:1]).then_inc(sqrt_done, 1)
                elif item[0] == "x1T":
                    g = item[1]
                    act.wait_ge(x1T_ps, g + 1)
                    act.activation(x1T[:, g, :, :], psA[g][:, :].rearrange("p (k t) -> p k t", k=2), ACT.Copy)\
                       .then_inc(x1T_copied, 1)
                elif item[0] == "xm":
                    g = item[1]
                    n_sqrt += 1
                    act.wait_ge(var_ready, n_sqrt)
                    act.activation(rstd[:, 2, GT * g:GT * g + GT], mv[:, 2, GT * g:GT * g + GT, 1], ACT.Sqrt,
                                   bias=eps[:, 0:1]).then_inc(sqrt_done, 1)
                elif item[0] == "x2T":
                    g = item[1]
                    act.wait_ge(x2T_ps, g + 1)
                    act.activation(x2T16[:, 0, :, TB * g:TB * g + TB],
                                   psA[g][:, :].rearrange("p (k t) -> p k t", k=2), ACT.Copy, scale=X_UP)\
                       .then_inc(x2hi_ready, 1)
                elif item[0] == "ffn":
                    g, n = item[1:]
                    s = NT * g + n
                    act.wait_ge(gate_done, s + 1)
                    if s >= 2:
                        act.wait_ge(inter_ready, s - 1)
                    act.activation(gelu[:, s % 2, :], gate_ps[s % 2], ACT.Gelu_apprx_tanh, scale=gm[:, 4, 0:1])\
                       .then_inc(gelu_done, 1)
                    act.wait_ge(inter_ready, s + 1)
                    act.activation(inter[g][:, 0, n, :], inter32[:, s % 2, :], ACT.Copy).then_inc(ihi_ready, 1)
                else:
                    g = item[1]
                    n_sqrt += 1
                    act.wait_ge(var_ready, n_sqrt)
                    act.activation(rstd[:, 3, GT * g:GT * g + GT], mv[:, 3, GT * g:GT * g + GT, 1], ACT.Sqrt,
                                   bias=eps[:, 0:1]).then_inc(sqrt_done, 1)

        @block.gpsimd
        def _(pool):
            pool.wait_ge(absmax, 1)
            pool.partition_all_reduce(gm[:, 1, :], gm[:, 0, :], P, RMAX).then_inc(allmax, 1)
            for s, (h, j) in enumerate(SCANS):
                pool.wait_ge(state_ready, 2 * s + 2)
                if s >= 3:
                    pool.wait_ge(sum_done, s - 2)
                pool.tensor_tensor(prod[:, s % 3, :], state[:, s % 3, :], vkrg[:, 2, h, :], ALU.mult)\
                    .then_inc(prod_ready, 1)
                d = piece_at(s)
                if d is not None:
                    w, e, f = PIECES[d]
                    if d == 0:
                        pool.wait_ge(scale_ready, 3)
                    if d >= 2:
                        pool.wait_ge(lo_ready, d - 1)
                        pool.wait_ge(hi_ready, d - 1)
                    pool.wait_ge(bits_ready, d + 1)
                    pool.tensor_tensor(full[:, d % 2, :], bits[:, 0, 0:1024].bitcast(F16),
                                       scales[:, w, 1024 * f:1024 * f + 1024], ALU.mult).then_inc(full_ready, 1)

        @block.tensor
        def _(pe):
            pe.wait_ge(loaded["wproj"], 16)
            for q in range(8):
                pe.wait_ge(mix_ready, q // 2 + 1)
                if q >= 2:
                    pe.wait_ge(proj_copied, q - 1)
                for t in range(2):
                    for k in range(2):
                        mm = pe.matmul(psA[q % 2][:, TB * t:TB * t + TB], wproj[:, q // 2, k, P * (q % 2):P * (q % 2) + P],
                                       mix[:, (q // 2) % 2, k, TB * t:TB * t + TB], start=(k == 0), stop=(k == 1))
                mm.then_inc(proj_done, 1)
            pe.wait_ge(loaded["ctxT"], 16)
            pe.wait_ge(loaded["wqk"], 16)
            for m in range(2):
                pe.wait_ge(proj_copied, 7 + m)
                for t in range(2):
                    mm = pe.matmul(psA[m][:, TB * t:TB * t + TB], wqk[:, m, :], ctxT[:, TB * t:TB * t + TB],
                                   start=True, stop=True)
                mm.then_inc(qk_ps, 1)
            pe.wait_ge(qk_copied, 2)
            for n in range(TILES):
                mm = pe.matmul(psA[n // 4][:, (n % 4) * 256:(n % 4) * 256 + 256], queryT[:, P * n:P * n + P],
                               keyT[:, T * (n // 2):T * (n // 2) + T], start=True, stop=True)
            mm.then_inc(energy_done, 1)
            pe.wait_ge(loaded["const"], 16)
            for i in range(2):
                pe.wait_ge(att_ready, 4 * i + 4)
                for n in range(4):
                    for k in range(2):
                        mm = pe.transpose(psA[i][:, (2 * n + k) * P:(2 * n + k + 1) * P],
                                          att[:, 4 * i + n, P * k:P * k + P], ident)
                mm.then_inc(attT_ps, 1)

            def spread(i):
                h, j = STEPS[i]
                if i < 2:
                    pe.wait_ge(attT_copied, i + 1)
                else:
                    pe.wait_ge(spread_used, i - 1)
                if j is None:
                    pe.wait_ge(mix_ready, 5 + h)
                for t in range(2):
                    lhs, rhs = (head_sum, diag) if j is None else (bcast[:, j, :], vkrg[:, 0, h, :])
                    mm = pe.matmul(psA[i % 2][:, TB * t:TB * t + TB], lhs, rhs[:, TB * t:TB * t + TB],
                                   start=True, stop=True)
                mm.then_inc(spread_done, 1)

            pe.wait_ge(bcast_ready, D)
            spread(0)
            spread(1)
            for s, (h, j) in enumerate(SCANS):
                i = STEPS.index((h, j))
                if j < D - 1:
                    spread(i + 1)
                pe.wait_ge(prod_ready, s + 1)
                if j == 0 and h:
                    pe.wait_ge(half_read, h)
                for t in range(2):
                    mm = pe.matmul(psO[:, TB * t:TB * t + TB], head_pick[:, 8 * (15 - j):8 * (15 - j) + P],
                                   prod[:, s % 3, TB * t:TB * t + TB], start=(j == 0), stop=(j == D - 1))
                mm.then_inc(sum_done, 1)
                if j == D - 1 and h + 1 < HALVES:
                    spread(i + 1)
                    spread(i + 2)

            for item in PLAN:
                if item[0] == "y":
                    g = item[1]
                    pe.wait_ge(loaded["wo"], 16)
                    pe.wait_ge(og_ready, 2)
                    for n in range(GT):
                        for k in range(2):
                            mm = pe.matmul(psA[g][:, n * 256:n * 256 + 256], og[:, k, (GT * g + n) * P:(GT * g + n + 1) * P],
                                           wo[:, k, :], start=(k == 0), stop=(k == 1))
                    mm.then_inc(y_done, 1)
                elif item[0] == "x1T":
                    g = item[1]
                    pe.wait_ge(x1_ready, g + 1)
                    for k in range(2):
                        for n in range(GT):
                            mm = pe.transpose(psA[g][:, k * TB + n * P:k * TB + n * P + P],
                                              x1[:, GT * g + n, P * k:P * k + P], ident)
                    mm.then_inc(x1T_ps, 1)
                elif item[0] == "xm":
                    g = item[1]
                    pe.wait_ge(x1T_copied, g + 1)
                    for n in range(GT):
                        b = (GT * g + n) // 2
                        for k in range(2):
                            mm = pe.matmul(psA[g][:, n * 256:n * 256 + 256], x1T[:, g, k, n * P:n * P + P],
                                           attT[:, k, 2 * b:2 * b + 2, :], start=(k == 0), stop=(k == 1))
                    mm.then_inc(xm_done, 1)
                elif item[0] == "x2T":
                    g = item[1]
                    pe.wait_ge(x2_ready, g + 1)
                    for k in range(2):
                        for n in range(GT):
                            mm = pe.transpose(psA[g][:, k * TB + n * P:k * TB + n * P + P],
                                              x2[:, GT * g + n, k:C:2], ident)
                    mm.then_inc(x2T_ps, 1)
                elif item[0] == "ffn":
                    g, n = item[1:]
                    s = NT * g + n
                    if n == 0:
                        pe.wait_ge(x2lo_ready, g + 1)
                        pe.wait_ge(lo_ready, NP)
                    for w, ps, done, used in ((0, gate_ps, gate_done, gelu_done), (1, up_ps, up_done, inter_ready)):
                        if s >= 2:
                            pe.wait_ge(used, s - 1)
                        passes = [(k, a, b) for k in range(2) for a, b in ((0, 0), (0, 1), (1, 0))]
                        for i, (k, a, b) in enumerate(passes):
                            mm = pe.matmul(ps[s % 2], w16[:, w, k, a, n * P:n * P + P],
                                           x2T16[:, b, k, TB * g:TB * g + TB], start=(i == 0), stop=(i == 5))
                        mm.then_inc(done, 1)
                else:
                    g = item[1]
                    pe.wait_ge(ilo_ready, NT * (g + 1))
                    for n in range(GT):
                        passes = [(m, a, b) for m in range(NT) for a, b in ((0, 0), (0, 1), (1, 0))]
                        for i, (m, a, b) in enumerate(passes):
                            mm = pe.matmul(psA[g][:, n * 256:n * 256 + 256], inter[g][:, a, m, n * P:n * P + P],
                                           w16[:, 2, m % 2, b, (m // 2) * 256:(m // 2) * 256 + 256],
                                           start=(i == 0), stop=(i == len(passes) - 1))
                    mm.then_inc(down_done, 1)

        @block.vector
        def _(dve):
            made = [0]

            def step(ins):
                made[0] += 1
                ins.then_inc(vec, 1)
                return made[0]

            def after(n):
                dve.wait_ge(vec, n)

            step(dve.memset(keep[:, :], 1.0))
            after(made[0])
            for b in range(2):
                step(dve.memset(keep[:, T * b:T * b + 1], 0.0))
            step(dve.memset(eps[:, :], EPS))
            dve.wait_ge(loaded["xT"], 16)
            for h in range(2):
                xb = xT[:, h, :].rearrange("p (b t) -> p b t", b=B)
                xxb = xx[:, h, :].rearrange("p (b t) -> p b t", b=B)
                step(dve.tensor_tensor(xxb[:, :, 1:T], xb[:, :, 0:T - 1], xb[:, :, 1:T], ALU.subtract))
                step(dve.tensor_tensor(xxb[:, :, 0:1], xb[:, :, 1:2], xb[:, :, 0:1], ALU.subtract))
            after(made[0])
            dve.wait_ge(loaded["cvec"], 16)
            for m in range(4):
                if m >= 2:
                    dve.wait_ge(proj_done, 2 * (m - 1))
                for h in range(2):
                    ins = dve.scalar_tensor_tensor(out=mix[:, m % 2, h, :], in0=xx[:, h, :], scalar=cvec[:, h, m:m + 1],
                                                   in1=xT[:, h, :], op0=ALU.mult, op1=ALU.add)
                ins.then_inc(mix_ready, 1)
                if m == 1:
                    dve.wait_ge(loaded["const"], 16)
                    for j in range(D):
                        dve.tensor_scalar(bcast[:, j, :], head_spread, lane[:, j:j + 1], None, ALU.mult)\
                           .then_inc(bcast_ready, 1)
            dve.wait_ge(loaded["flat"], 16)
            dve.tensor_reduce(gm[:, 0, :], flat[:, :, :], AX.X, ALU.max, apply_absolute_value=True).then_inc(absmax, 1)
            dve.wait_ge(loaded["packed"], 16)
            for w in range(3):
                dve.tensor_copy(p16[:, w, :], packed_sb[:, w, :].bitcast(U16)[:, 0:4096:2]).then_inc(p16_ready, 1)
            dve.wait_ge(allmax, 1)
            step(dve.tensor_scalar(gm[:, 1, :], gm[:, 1, :], 2.0 ** -60, None, ALU.max))
            after(made[0])
            step(dve.tensor_scalar(gm[:, 2, :].bitcast(I32), gm[:, 1, :].bitcast(I32), 0x7F800000, None, ALU.bitwise_and))
            after(made[0])
            step(dve.reciprocal(gm[:, 5, :], gm[:, 2, :]))
            after(made[0])
            dve.tensor_scalar(gm[:, 3, :], gm[:, 5, :], W_UP * CODE_UP, None, ALU.mult).then_inc(gready, 1)
            step(dve.tensor_scalar(gm[:, 4, 0:1], gm[:, 2, 0:1], 1.0 / (X_UP * W_UP), None, ALU.mult))
            step(dve.tensor_scalar(gm[:, 4, 1:2], gm[:, 5, 0:1], I_DOWN / (X_UP * W_UP), None, ALU.mult))
            step(dve.tensor_tensor(gm[:, 6, 0:1], gm[:, 2, 0:1], gm[:, 2, 1:2], ALU.mult))
            after(made[0])
            step(dve.tensor_scalar(gm[:, 4, 2:3], gm[:, 6, 0:1], gm[:, 2, 2:3], 1.0 / (I_DOWN * W_UP), ALU.mult, ALU.mult))
            dve.wait_ge(energy_done, 1)
            for i in range(2):
                ins = dve.tensor_reduce(smax[:, 0, 4 * i:4 * i + 4], psA[i][:, :].rearrange("p (n k) -> p n k", n=4),
                                        AX.X, ALU.max, negate=True)
                if i == 0:
                    step(ins)
                    after(made[0])
            ins.then_inc(negmax_ready, 1)
            dve.wait_ge(exp_done, TILES)
            step(dve.reciprocal(smax[:, 2, :], smax[:, 1, :]))
            after(made[0])
            for n in range(TILES):
                dve.tensor_scalar(att[:, n, :], att[:, n, :], smax[:, 2, n:n + 1], None, ALU.mult).then_inc(att_ready, 1)

            dve.wait_ge(decay_ready, 1)
            dve.wait_ge(proj_copied, 8)
            for s in range(2):
                kvb = kv[:, s, :].rearrange("p (b t) -> p b t", b=B)
                step(dve.memset(kvb[:, :, 0:1], 0.0))
            kv_at = {}

            def make_diag(h):
                if h:
                    dve.wait_ge(half_read, h)
                dve.scalar_tensor_tensor(out=diag, in0=vkrg[:, 1, h, :], scalar=cvec[:, h, 5:6],
                                         in1=vkrg[:, 2, h, :], op0=ALU.mult, op1=ALU.mult).then_inc(mix_ready, 1)

            def make_kv(s):
                h, j = SCANS[s]
                i = STEPS.index((h, j))
                dve.wait_ge(spread_done, i + 1)
                kvb = kv[:, s % 2, :].rearrange("p (b t) -> p b t", b=B)
                vb = psA[i % 2][:, :].rearrange("p (b t) -> p b t", b=B)
                kb = vkrg[:, 1, h, :].rearrange("p (b t) -> p b t", b=B)
                dve.tensor_tensor(kvb[:, :, 1:T], vb[:, :, 0:T - 1], kb[:, :, 0:T - 1], ALU.mult).then_inc(spread_used, 1)
                kv_at[s] = i + 1

            def diag_v(h):
                i = STEPS.index((h, None))
                dve.wait_ge(spread_done, i + 1)
                dve.tensor_tensor(diag, psA[i % 2][:, :], vkrg[:, 0, h, :], ALU.mult).then_inc(spread_used, 1)

            make_diag(0)
            diag_v(0)
            step(dve.tensor_scalar(psW[:, :], keep[:, :], decay[:, 0, 1:2], None, ALU.mult))
            decay_at = made[0]
            make_kv(0)
            for s, (h, j) in enumerate(SCANS):
                if s + 1 < len(SCANS) and SCANS[s + 1][0] == h:
                    make_kv(s + 1)
                dve.wait_ge(spread_used, kv_at[s])
                after(decay_at)
                if s >= 3:
                    dve.wait_ge(prod_ready, s - 2)
                for t in range(2):
                    dve.tensor_tensor_scan(state[:, s % 3, TB * t:TB * t + TB], psW[:, :],
                                           kv[:, s % 2, TB * t:TB * t + TB], 0.0, ALU.mult, ALU.add)\
                       .then_inc(state_ready, 1)
                d = piece_at(s)
                if d is not None:
                    if d >= 1:
                        low_part(dve, d - 1, full_ready, hi_ready, lo_ready, w16, full, PIECES)
                    w, e, f = PIECES[d]
                    if d == 0:
                        dve.wait_ge(p16_ready, 3)
                    src = p16[:, w, 1024 * f:1024 * f + 1024]
                    step(dve.tensor_scalar(bits[:, 1, 0:1024], src, 9 - 4 * e, 0x0E00, ALU.logical_shift_left, ALU.bitwise_and))
                    step(dve.tensor_scalar(bits[:, 0, 0:1024], src, 12 - 4 * e, 0x8000, ALU.logical_shift_left, ALU.bitwise_and))
                    after(made[0])
                    dve.tensor_tensor(bits[:, 0, 0:1024], bits[:, 0, 0:1024], bits[:, 1, 0:1024], ALU.bitwise_or)\
                       .then_inc(bits_ready, 1)
                if j == D - 1:
                    dve.wait_ge(sum_done, s + 1)
                    dve.tensor_tensor(og[:, h, :], psO[:, :], diag, ALU.add).then_inc(half_read, 1)
                    dve.wait_ge(half_read, h + 1)
                    dve.tensor_tensor(og[:, h, :], og[:, h, :], vkrg[:, 3, h, :], ALU.mult).then_inc(og_ready, 1)
                    if h + 1 < HALVES:
                        dve.wait_ge(state_ready, 2 * s + 2)
                        step(dve.tensor_scalar(psW[:, :], keep[:, :], decay[:, h + 1, 1:2], None, ALU.mult))
                        decay_at = made[0]
                        make_diag(h + 1)
                        diag_v(h + 1)
                        make_kv(s + 1)
            low_part(dve, NP - 1, full_ready, hi_ready, lo_ready, w16, full, PIECES)

            def stats(i, tiles, srcs):
                for n, src in zip(tiles, srcs):
                    step(dve.bn_stats(lnst[:, n % 2, :], src))
                    after(made[0])
                    ins = dve.bn_aggr(mv[:, i, n, :], lnst[:, n % 2, :])
                    if n != tiles[-1]:
                        step(ins)
                ins.then_inc(var_ready, 1)

            sqrts = [0]

            def scale_rows(i, g):
                sqrts[0] += 1
                dve.wait_ge(sqrt_done, sqrts[0])
                step(dve.reciprocal(rstd[:, i, GT * g:GT * g + GT], rstd[:, i, GT * g:GT * g + GT]))
                after(made[0])

            def normalize(i, n, dst, src):
                return dve.tensor_scalar(dst, src, mv[:, i, n, 0:1], rstd[:, i, n:n + 1], ALU.subtract, ALU.mult)

            dve.wait_ge(loaded["xtok"], 16)
            dve.wait_ge(loaded["ln"], 16)
            for item in PLAN:
                g = item[1]
                tiles = list(range(GT * g, GT * g + GT))
                cols = [psA[g][:, (n % GT) * 256:(n % GT) * 256 + 256] for n in tiles]
                zt = ztmp[:, GT * g:GT * g + GT, :]
                if item[0] == "y":
                    dve.wait_ge(y_done, g + 1)
                    stats(0, tiles, cols)
                    scale_rows(0, g)
                    for n, src in zip(tiles, cols):
                        step(normalize(0, n, ztmp[:, n, :], src))
                    after(made[0])
                    step(dve.tensor_tensor(zt, zt, ln[:, 0:1, :].broadcast_to([P, GT, C]), ALU.mult))
                    after(made[0])
                    step(dve.tensor_tensor(zt, zt, ln[:, 1:2, :].broadcast_to([P, GT, C]), ALU.add))
                    after(made[0])
                    step(dve.tensor_tensor(zt, zt, xtok[:, GT * g:GT * g + GT, :], ALU.add))
                    after(made[0])
                    stats(1, tiles, [ztmp[:, n, :] for n in tiles])
                    scale_rows(1, g)
                    for n in tiles:
                        ins = normalize(1, n, x1[:, n, :], ztmp[:, n, :])
                        if n != tiles[-1]:
                            step(ins)
                    ins.then_inc(x1_ready, 1)
                elif item[0] == "xm":
                    dve.wait_ge(xm_done, g + 1)
                    dve.wait_ge(x1_ready, g + 1)
                    step(dve.tensor_tensor(zt, psA[g][:, :].rearrange("p (n c) -> p n c", n=GT), x1[:, GT * g:GT * g + GT, :], ALU.add))
                    after(made[0])
                    stats(2, tiles, [ztmp[:, n, :] for n in tiles])
                    scale_rows(2, g)
                    for n in tiles:
                        ins = normalize(2, n, x2[:, n, :], ztmp[:, n, :])
                        if n != tiles[-1]:
                            step(ins)
                    ins.then_inc(x2_ready, 1)
                elif item[0] == "x2T":
                    dve.wait_ge(x2hi_ready, g + 1)
                    dve.scalar_tensor_tensor(out=x2T16[:, 1, :, TB * g:TB * g + TB],
                                             in0=psA[g][:, :].rearrange("p (k t) -> p k t", k=2), scalar=X_UP,
                                             in1=x2T16[:, 0, :, TB * g:TB * g + TB], op0=ALU.mult, op1=ALU.subtract)\
                       .then_inc(x2lo_ready, 1)
                elif item[0] == "ffn":
                    n = item[2]
                    s = NT * g + n
                    dve.wait_ge(gelu_done, s + 1)
                    dve.wait_ge(up_done, s + 1)
                    if s >= 2:
                        dve.wait_ge(ilo_ready, s - 1)
                        dve.wait_ge(ihi_ready, s - 1)
                    dve.scalar_tensor_tensor(out=inter32[:, s % 2, :], in0=up_ps[s % 2], scalar=gm[:, 4, 1:2],
                                             in1=gelu[:, s % 2, :], op0=ALU.mult, op1=ALU.mult).then_inc(inter_ready, 1)
                    dve.wait_ge(ihi_ready, s + 1)
                    dve.tensor_tensor(inter[g][:, 1, n, :], inter32[:, s % 2, :], inter[g][:, 0, n, :], ALU.subtract)\
                       .then_inc(ilo_ready, 1)
                elif item[0] == "down":
                    dve.wait_ge(down_done, g + 1)
                    fg = ff[:, GT * g:GT * g + GT, :]
                    step(dve.scalar_tensor_tensor(out=fg.rearrange("p n c -> p (n c)"), in0=psA[g][:, :], scalar=gm[:, 4, 2:3],
                                                  in1=x2[:, GT * g:GT * g + GT, :].rearrange("p n c -> p (n c)"),
                                                  op0=ALU.mult, op1=ALU.add))
                    after(made[0])
                    stats(3, tiles, [ff[:, n, :] for n in tiles])
                    scale_rows(3, g)
                    for n in tiles:
                        ins = normalize(3, n, ztmp[:, n, :], ff[:, n, :])
                        if n != tiles[-1]:
                            step(ins)
                    ins.then_inc(ff_ready, 1)


def low_part(dve, d, full_ready, hi_ready, lo_ready, w16, full, pieces):
    w, e, f = pieces[d]
    dve.wait_ge(full_ready, d + 1)
    dve.wait_ge(hi_ready, d + 1)
    cols = slice(1024 * f, 1024 * f + 1024)
    dve.tensor_tensor(w16[:, w, e, 1, cols], full[:, d % 2, :], w16[:, w, e, 0, cols], ALU.subtract)\
       .then_inc(lo_ready, 1)


def kernel(**inputs):
    import numpy as np
    import concourse.bacc as bacc
    from concourse.bass_utils import run_bass_kernel_spmd

    a = {k: np.asarray(v) for k, v in inputs.items()}
    n, c = N, C

    def hidden_order(w):
        return w.reshape(w.shape[0], 8, P, 2).transpose(0, 1, 3, 2).reshape(w.shape[0], MLP)

    x = a["x"].reshape(n, c)
    gate, up, down = (a[f"L0_ffn_{m}_W_packed"] for m in ("gate", "up", "down"))
    sg, su, sd = (a[f"L0_ffn_{m}_scales"] for m in ("gate", "up", "down"))
    lanes = np.arange(P)
    to_sum = (lanes[:, None] // D == lanes[None, :] % 8).astype(np.float32)
    pick = np.zeros((P, 248), np.float32)
    pick[lanes, 120 + lanes // D] = 1.0
    consts = np.concatenate([np.eye(P, dtype=np.float32), to_sum, pick, to_sum.T,
                             (lanes[:, None] // 8 == np.arange(D)[None, :]).astype(np.float32)], axis=1)

    def dim_major(w):
        return w.reshape(2, 8, D, -1).transpose(0, 2, 1, 3).reshape(c, -1)
    data = {
        "x_chan": x.T,
        "x_tok": x,
        "ctx_chan": a["ctx_1024"].reshape(n, P).T,
        "w_chan": np.stack([dim_major(a["L0_attn_Wv"]).T, a["L0_attn_Wk"].T, a["L0_attn_Wr"].T,
                            dim_major(a["L0_attn_Wg"]).T, dim_major(a["L0_attn_Wo"].T)]),
        "chan_vecs": np.stack([a["L0_attn_tm_" + m] for m in "vkrg"] + [a["L0_attn_time_decay"].reshape(c),
                              a["L0_attn_time_first"].reshape(c)], axis=1),
        "ln_vecs": np.stack([a["L0_attn_ln_w"], a["L0_attn_ln_b"]]),
        "xq_chan": np.stack([a["L0_xattn_Wq"].T, a["L0_xattn_Wk"].T]),
        "xq_bias": np.stack([a["L0_xattn_bq"], a["L0_xattn_bk"]], axis=1),
        "packed": np.stack([hidden_order(gate.T), hidden_order(up.T),
                            down.T.reshape(8, P, c).transpose(1, 0, 2).reshape(P, MLP)]),
        "scale_rows_in": np.stack([hidden_order(sg.T), hidden_order(su.T)]),
        "scale_rows_out": sd.T.reshape(8, 8, c),
        "scale_flat": np.stack([sg.reshape(-1), su.reshape(-1), sd.reshape(-1)]),
        "consts": consts,
    }
    nc = bacc.Bacc("TRN2", target_bir_lowering=False, num_devices=1)
    arrays, args = {}, []
    for name, value in data.items():
        value = np.ascontiguousarray(value)
        arrays[name] = value
        args.append(nc.dram_tensor(name, value.shape, mybir.dt.from_np(value.dtype), kind="ExternalInput").ap())
    args.append(nc.dram_tensor("out", (n, c), F32, kind="ExternalOutput").ap())
    decoder_layer(nc, *args)
    result = run_bass_kernel_spmd(nc, [arrays], core_ids=[0])
    return result.results[0]["out"].reshape(B, T, C)
```

```python
from contextlib import ExitStack

import concourse.bass as bass
from concourse import mybir

ALU = mybir.AluOpType
ACT = mybir.ActivationFunctionType
F32 = mybir.dt.float32
F16 = mybir.dt.float16
BF16 = mybir.dt.bfloat16
I32 = mybir.dt.int32
U32 = mybir.dt.uint32
U16 = mybir.dt.uint16
AX = mybir.AxisListType
RMAX = bass.bass_isa.ReduceOp.max

P = 128
B, T, C = 4, 256, 256
N = B * T
D = 16
HPH = P // D
GROUPS = 2
TB = N // GROUPS
GT = TB // P
TILES = N // P
MLP = 2048
NT = MLP // P
PC = 512
EPS = 1e-5
X_UP = 2048.0
W_UP = 4096.0
I_DOWN = 2.0 ** -8
CODE_UP = 2.0 ** 14

V, K, R, G = range(4)
SLOT = {K: 0, R: 1, G: 2, V: 3}
UNITS = [(V, 0, 0), (K, 0, 0), (R, 0, 0), (V, 0, 1), (K, 0, 1), (R, 0, 1), (G, 0, 0), (G, 0, 1)]
UNITS += [(m, 1, h) for m in (V, K, R, G) for h in range(2)]
MIXES = [(m, g) for g in range(GROUPS) for m in (V, K, R, G)]
PASSES = [(g, h) for g in range(GROUPS) for h in range(2)]
SCANS = [(q, j) for q in range(len(PASSES)) for j in range(D)]
SPREADS = [(q, j) for q in range(len(PASSES)) for j in [None] + list(range(D))]
PIECES = [(w, e, f) for w in range(3) for e in range(2) for f in range(2048 // PC)]
UPPIECES = 2 * len(PIECES) // 3


def make_plan():
    plan = [("xx", 0), ("mix", 0), ("mix", 1), ("mix", 2), ("proj", 0), ("parts", 0), ("proj", 1), ("proj", 2),
            ("diag", 0), ("spread", 0), ("spread", 1), ("use", 0), ("spread", 2), ("use", 1)]
    beside = {s: [] for s in range(len(SCANS))}
    beside[0] += [("proj", 3), ("xx", 1), ("mix", 3)]
    beside[1] += [("proj", 4), ("parts", 1), ("mix", 4)]
    beside[2] += [("proj", 5), ("mix", 5)]
    beside[3] += [("proj", 6), ("mix", 6)]
    beside[4] += [("proj", 7)]
    beside[5] += [("mix", 7)]
    for u in range(8, 16):
        beside[u - 2] += [("proj", u)]
    beside[6] += [("codes", 0)]
    beside[7] += [("parts", 2), ("codes", 1)]
    beside[8] += [("parts", 3), ("codes", 2), ("G",)]
    beside[9] += [("scale", 0)]
    beside[11] += [("scale", 1)]
    for d in range(UPPIECES):
        beside[11 + d] += [("piece", d)]
        beside[13 + d] += [("low", d)]
    for i in range(4):
        beside[15 + i] += [("qk", i)]
        beside[20 + i] += [("energy", i)]
        beside[22 + i] += [("exp", i)]
        beside[28 + i] += [("attT", i)]
    beside[26] += [("rowsum",)]
    beside[27] += [("norm",)]
    beside[36] += [("y", 0)]
    beside[39] += [("aff0", 0)]
    beside[40] += [("stat0", 0)]
    beside[42] += [("rows0", 0)]
    beside[44] += [("aff", 0)]
    beside[49] += [("stat1", 0)]
    beside[51] += [("rows1", 0)]
    beside[53] += [("x1T", 0)]
    beside[55] += [("xm", 0)]
    beside[59] += [("stat2", 0)]
    beside[61] += [("rows2", 0)]
    beside[63] += [("x2T", 0), ("x2lo", 0)]
    for s, (q, j) in enumerate(SCANS):
        here = SPREADS.index((q, j))
        upto = SPREADS.index(SCANS[s + 1]) if s + 1 < len(SCANS) else here
        for i in range(here + 1, upto + 1):
            if i + 1 < len(SPREADS):
                plan.append(("spread", i + 1))
            plan.append(("use", i))
        plan += [("scan", s)]
        if s:
            plan.append(("sum", s - 1))
        if j == 2 and q:
            plan.append(("fin", q - 1))
        if j == 8 and q + 1 < len(PASSES):
            plan.append(("diag", q + 1))
        plan += beside[s]
    plan += [("sum", len(SCANS) - 1), ("fin", len(PASSES) - 1)]
    after = {0: [("y", 1), ("aff0", 1)], 1: [("scale", 2), ("stat0", 1)], 2: [("rows0", 1), ("aff", 1)], 5: [("stat1", 1)],
             6: [("rows1", 1)], 7: [("x1T", 1), ("xm", 1)], 9: [("stat2", 1)], 10: [("rows2", 1)], 11: [("x2T", 1), ("x2lo", 1)]}
    down_pieces = list(range(UPPIECES, len(PIECES)))
    for n in range(NT):
        plan.append(("ffn", 0, n))
        if n >= 3 and n - 3 < len(down_pieces):
            plan.append(("piece", down_pieces[n - 3]))
        if 4 <= n < 4 + len(down_pieces):
            plan.append(("low", down_pieces[n - 4]))
        plan += after.get(n, [])
    plan += [("ffn", 1, 0), ("ffn", 1, 1)]
    plan += [("down", 0), ("ffn", 1, 2), ("out", 0)]
    plan += [("ffn", 1, n) for n in range(3, NT)] + [("down", 1), ("out", 1)]
    return plan


PLAN = make_plan()
JOBS = [item for item in PLAN if item[0] in ("proj", "qk", "energy", "attT")]


def decoder_layer(nc, x_chan, x_tok, ctx_chan, w_chan, chan_vecs, ln_vecs, xq_chan, xq_bias,
                  packed, scale_rows_in, scale_rows_out, scale_flat, consts, out):
    with ExitStack() as stack:
        def sb(name, shape, dt=F32):
            return stack.enter_context(nc.sbuf_tensor(name, shape, dt))

        def sem(name):
            return stack.enter_context(nc.semaphore(name))

        region_a = sb("region_a", [P, 8192])
        xT = region_a[:, 0:2048].rearrange("p (h t) -> p h t", h=2)
        xx = region_a[:, 2048:4096].rearrange("p (h t) -> p h t", h=2)
        mix = region_a[:, 4096:8192].rearrange("p (m h t) -> p m h t", m=4, h=2)
        bits = region_a[:, 0:768].bitcast(U16).rearrange("p (s n) -> p s n", s=3)
        full = region_a[:, 1024:2048].rearrange("p (s n) -> p s n", s=2)
        xtok = region_a[:, 6144:8192].rearrange("p (n c) -> p n c", n=TILES)
        region_b = sb("region_b", [P, 8192])
        proj = region_b[:, :].rearrange("p (m h t) -> p m h t", m=4, h=2)
        og = proj[:, SLOT[V]]
        inter = [r[:, :].bitcast(F16).rearrange("p (m n t) -> p m n t", m=2, n=NT) for r in (region_b, region_a)]
        region_c = sb("region_c", [P, 8192])
        kv = region_c[:, 0:1024].rearrange("p (s t) -> p s t", s=2)
        state = region_c[:, 1024:3072].rearrange("p (s t) -> p s t", s=4)
        prod = region_c[:, 3072:5120].rearrange("p (s t) -> p s t", s=4)
        flat = region_c[:, 4608:4992].rearrange("p (w n) -> p w n", w=3)
        vparts = region_c[:, 5120:8192].bitcast(BF16).rearrange("p (u m t) -> p u m t", u=4, m=3)
        ztmp = region_c[:, 5120:7168].rearrange("p (n c) -> p n c", n=TILES)
        x1T = region_c[:, 7168:8192].rearrange("p (k t) -> p k t", k=2)
        gelu = region_c[:, 0:1024].rearrange("p (s t) -> p s t", s=2)
        inter32 = region_c[:, 1024:2048].rearrange("p (s t) -> p s t", s=2)
        ff = region_c[:, 2048:4096].rearrange("p (n c) -> p n c", n=TILES)

        w16 = sb("w16", [P, 3, 2, 2, 2048], F16)
        wproj = w16[:, 1, 0].rearrange("p m n -> p (m n)").bitcast(F32).rearrange("p (m k n) -> p m k n", m=4, k=2)
        packed_in = w16[:, 0].rearrange("p e m n -> p (e m n)").bitcast(I32).rearrange("p (w n) -> p w n", w=2)
        packed_down = w16[:, 1, 1].rearrange("p m n -> p (m n)").bitcast(I32)
        early = w16[:, 2].rearrange("p e m n -> p (e m n)").bitcast(F32)
        ctxT = early[:, 0:1024]
        queryT = early[:, 1024:2048]
        keyT = early[:, 2048:3072]
        wqk = early[:, 3072:3328].rearrange("p (m n) -> p m n", m=2)
        diag = early[:, 3328:3840]
        p16 = sb("p16", [P, 3, 2048], U16)
        scales = sb("scales", [P, 3, 2048])
        x1 = scales[:, 0, :].rearrange("p (n c) -> p n c", n=TILES)
        x2 = scales[:, 1, :].rearrange("p (n c) -> p n c", n=TILES)
        att = scales[:, 2, :].rearrange("p (n k) -> p n k", n=TILES)
        x2T16 = p16[:, 0:2, :].bitcast(F16).rearrange("p m (k t) -> p m k t", k=2)
        attT = sb("attT", [P, 2, TILES, P])
        vstack = [sb("vstack0", [96, 4, N], BF16),
                  region_a[0:96, 2048:4096].bitcast(BF16).rearrange("p (q t) -> p q t", q=4)]
        const = sb("const", [P, 636])
        ident = const[:, 0:128]
        head_sum = const[:, 128:256]
        head_pick = const[:, 256:504]
        head_spread = const[:, 504:632]
        lane = const[:, 632:636]
        spread_w = sb("spread_w", [96, 4, P], BF16)
        keep = sb("keep", [P, TB])
        rest = keep
        wo = sb("wo", [P, 2, C])
        ln = sb("ln", [P, 2, C])
        cvec = sb("cvec", [P, 2, 6])
        decay = sb("decay", [P, 2, 2])
        qkb = sb("qkb", [P, 2])
        gm = sb("gm", [P, 8, 3])
        smax = sb("smax", [P, 3, TILES])
        lnst = sb("lnst", [P, 2, 6])
        mv = sb("mv", [P, 4, TILES, 2])
        rstd = sb("rstd", [P, 4, TILES])
        shift = sb("shift", [P, 4, TILES])
        eps = sb("eps", [P, 1])

        psA = [stack.enter_context(nc.psum_tensor(f"psA{i}", [P, 1024], F32)) for i in range(2)]
        psB = stack.enter_context(nc.psum_tensor("psB", [P, 4, TB], F32))
        job_ps = [psA[0][:, 0:TB], psA[0][:, TB:1024]]
        spread_ps = [psB[:, 0, :], psB[:, 1, :]]
        sum_ps = [psB[:, 2, :], psB[:, 3, :]]
        gate_ps = [psB[:, 0, :], psB[:, 2, :]]
        up_ps = [psB[:, 1, :], psB[:, 3, :]]
        decay_ps = psA[1]

        loads = ["x0", "x1", "cvec", "wv", "wk", "wr", "wg", "const", "ctx", "wqk", "qkb", "packed_in", "packed_down",
                 "flat", "scales_in", "scales_out", "wo", "ln", "xtok"]
        loaded = {n: sem("loaded_" + n) for n in loads}
        stacked = [[sem(f"stacked{u}_{quad}") for quad in range(4)] for u in range(4)]
        vec = sem("vec_steps")
        act_steps = sem("act_steps")
        pool_steps = sem("pool_steps")
        names = """mix_ready job_done job_used decay_set spread_w_ready high_ready mid_ready rest1_ready rest2_ready
            diag_ready spread_done spread_used state_ready prod_ready sum_done half_read og_ready
            absmax allmax g_ready scale_ready codes_ready bits_ready full_ready hi_ready lo_ready
            negmax_ready exp_done recip_ready att_ready y_done var_ready sqrt_done rows_ready
            normal_ready xlb_ready z_ready x1T_done x1T_ready xm_done x2T_done x2hi_ready x2lo_ready
            gate_done up_done gelu_done inter_ready ihi_ready ilo_ready down_done stored""".split()
        S = {n: sem(n) for n in names}

        def vp_weight(m):
            return ("wv", "wk", "wr", "wg")[m]

        def unit_no(m, g, h):
            return UNITS.index((m, g, h))

        def used_jobs(u):
            return JOBS.index(("proj", u)) + 1

        def og_cols(q):
            g, h = PASSES[q]
            return og[:, h, TB * g:TB * g + TB]

        def unit(m, q):
            g, h = PASSES[q]
            return proj[:, SLOT[m], h, TB * g:TB * g + TB]

        def tiles_of(g):
            return list(range(GT * g, GT * g + GT))

        def ps_tile(g, n):
            return psA[g][:, (n % GT) * C:(n % GT) * C + C]

        def down_tile(g, n):
            return ps_tile(g, n) if g == 0 else psA[n % GT // 2][:, n % 2 * TB:n % 2 * TB + C]

        def out_chunks(g):
            return [tiles_of(g)] if g == 0 else [[n] for n in tiles_of(g)]

        NORMS = []
        for item in PLAN:
            if item[0] in ("stat0", "stat1", "stat2"):
                NORMS.append((int(item[0][-1]), item[1], tiles_of(item[1])))
            elif item[0] == "out":
                NORMS += [(3, item[1], tiles) for tiles in out_chunks(item[1])]

        def norm_no(i, g, tiles=None):
            return NORMS.index((i, g, tiles or tiles_of(g)))

        def normals_before(i, g, tiles=None):
            return sum(len(t) for _, _, t in ACT_NORMS[:ACT_NORMS.index((i, g, tiles or tiles_of(g))) + 1])

        ACT_NORMS = []
        for item in PLAN:
            if item[0] in ("rows0", "rows1", "rows2"):
                ACT_NORMS.append((int(item[0][-1]), item[1], tiles_of(item[1])))
            elif item[0] == "out":
                ACT_NORMS += [(3, item[1], tiles) for tiles in out_chunks(item[1])]

        def normals(stage, tiles):
            return normals_before(3, stage[1], tiles)

        block = stack.enter_context(nc.Block())

        @block.sync
        def _(sp):
            def load(dst, src, name):
                sp.dma_start(dst, src).then_inc(loaded[name], 16)

            def load_x(g):
                load(xT[:, :, TB * g:TB * g + TB], x_chan.rearrange("(h p) t -> p h t", p=P)[:, :, TB * g:TB * g + TB],
                     f"x{g}")

            def load_w(m):
                load(wproj[:, m], w_chan[m].rearrange("(k p) n -> p k n", p=P), vp_weight(m))

            def stack_v(u):
                g, h = PASSES[u]
                sp.wait_ge(S["rest2_ready"], u + 1)
                if u == 1:
                    sp.wait_ge(S["mix_ready"], len(MIXES))
                for quad in range(4):
                    for m in range(3):
                        sp.dma_start(vstack[h][32 * m:32 * m + 32, quad, TB * g:TB * g + TB],
                                     vparts[32 * quad:32 * quad + 32, u, m, :]).then_inc(stacked[u][quad], 16)

            load_x(0)
            load(cvec[:, :, :], chan_vecs.rearrange("(h p) v -> p h v", p=P), "cvec")
            load_w(V)
            load_w(K)
            load(const[:, :], consts, "const")
            load_w(R)
            load_x(1)
            stack_v(0)
            load_w(G)
            load(packed_in, packed[0:2].rearrange("w p n -> p w n"), "packed_in")
            load(packed_down, packed[2], "packed_down")
            load(flat, scale_flat.rearrange("w (p n) -> p w n", p=P), "flat")
            stack_v(1)
            for w in range(2):
                for k in range(8):
                    load(scales[16 * k:16 * k + 16, w, :], scale_rows_in[w, k:k + 1, :].broadcast_to([16, 2048]),
                         "scales_in")
            stack_v(2)
            stack_v(3)
            load(ctxT, ctx_chan, "ctx")
            load(wqk, xq_chan.rearrange("m p n -> p m n"), "wqk")
            load(qkb[:, :], xq_bias, "qkb")
            load(wo[:, :, :], w_chan[4].rearrange("(k p) n -> p k n", p=P), "wo")
            load(ln[:, :, :], ln_vecs.partition_broadcast(P), "ln")
            sp.wait_ge(S["job_done"], used_jobs(len(UNITS) - 1))
            load(xtok, x_tok.rearrange("(n p) c -> p n c", p=P), "xtok")
            sp.wait_ge(S["job_used"], len(JOBS))
            for k in range(8):
                load(scales[16 * k:16 * k + 16, 2, :].rearrange("p (c n) -> p c n", c=8),
                     scale_rows_out[:, k, :].partition_broadcast(16), "scales_out")
            stores = 0
            for g in range(GROUPS):
                for tiles in out_chunks(g):
                    stores += 1
                    sp.wait_ge(S["normal_ready"], normals(("out", g), tiles))
                    sp.dma_start(out[P * tiles[0]:P * tiles[-1] + P].rearrange("(n p) c -> p n c", p=P),
                                 ztmp[:, tiles[0]:tiles[-1] + 1, :]).then_inc(S["stored"], 16)
            sp.wait_ge(S["stored"], 16 * stores)

        @block.scalar
        def _(act):
            steps = [0]

            def step(ins):
                steps[0] += 1
                ins.then_inc(act_steps, 1)

            def sqrt(i, g, tiles):
                act.wait_ge(S["var_ready"], norm_no(i, g, tiles) + 1)
                a, b = tiles[0], tiles[-1] + 1
                act.activation(rstd[:, i, a:b], mv[:, i, a:b, 1], ACT.Sqrt, bias=eps[:, 0:1]).then_inc(S["sqrt_done"], 1)

            def normalize(i, g, tiles, dst, src):
                act.wait_ge(S["rows_ready"], norm_no(i, g, tiles) + 1)
                for n in tiles:
                    act.activation(dst(n), src(n), ACT.Identity, bias=shift[:, i, n:n + 1], scale=rstd[:, i, n:n + 1])\
                       .then_inc(S["normal_ready"], 1)

            act.wait_ge(loaded["cvec"], 16)
            step(act.activation(decay[:, :, 0], cvec[:, :, 4], ACT.Exp))
            act.wait_ge(act_steps, steps[0])
            step(act.activation(decay[:, :, 1], decay[:, :, 0], ACT.Exp, scale=-1.0))
            act.wait_ge(act_steps, steps[0])
            act.wait_ge(vec, 3)
            for h in range(2):
                act.activation(decay_ps[:, TB * h:TB * h + TB], keep[:, :], ACT.Copy, scale=decay[:, h, 1:2])\
                   .then_inc(S["decay_set"], 1)

            for item in PLAN:
                kind = item[0]
                if kind in ("proj", "qk", "attT"):
                    job = JOBS.index(item)
                    act.wait_ge(S["job_done"], job + 1)
                    ps = job_ps[job % 2]
                if kind == "proj":
                    m, g, h = UNITS[item[1]]
                    act.activation(proj[:, SLOT[m], h, TB * g:TB * g + TB], ps, ACT.Sigmoid if m == G else ACT.Copy)\
                       .then_inc(S["job_used"], 1)
                elif kind == "parts":
                    u = item[1]
                    g, h = PASSES[u]
                    act.wait_ge(S["job_used"], used_jobs(unit_no(V, g, h)))
                    act.activation(vparts[:, u, 0, :], unit(V, u), ACT.Copy).then_inc(S["high_ready"], 1)
                    act.wait_ge(S["rest1_ready"], u + 1)
                    act.activation(vparts[:, u, 1, :], rest[:, :], ACT.Copy).then_inc(S["mid_ready"], 1)
                elif kind == "codes":
                    w = item[1]
                    act.wait_ge(loaded["packed_down" if w == 2 else "packed_in"], 16)
                    src = packed_down if w == 2 else packed_in[:, w, :]
                    act.activation(p16[:, w, :], src.bitcast(U16)[:, 0:4096:2], ACT.Copy).then_inc(S["codes_ready"], 1)
                elif kind == "scale":
                    w = item[1]
                    act.wait_ge(S["g_ready"], 1)
                    act.wait_ge(loaded["scales_out" if w == 2 else "scales_in"], 16 * (8 if w == 2 else 16))
                    act.activation(scales[:, w, :], scales[:, w, :], ACT.Copy, scale=gm[:, 3, w:w + 1])\
                       .then_inc(S["scale_ready"], 1)
                elif kind == "piece":
                    d = item[1]
                    w, e, f = PIECES[d]
                    act.wait_ge(S["full_ready"], d + 1)
                    if d == 0:
                        act.wait_ge(S["codes_ready"], 2)
                    act.activation(w16[:, w, e, 0, PC * f:PC * f + PC], full[:, d % 2, :], ACT.Copy)\
                       .then_inc(S["hi_ready"], 1)
                elif kind == "qk":
                    m, g = item[1] // 2, item[1] % 2
                    act.wait_ge(loaded["qkb"], 16)
                    act.activation((queryT, keyT)[m][:, TB * g:TB * g + TB], ps, ACT.Identity, bias=qkb[:, m:m + 1])\
                       .then_inc(S["job_used"], 1)
                elif kind == "exp":
                    i = item[1]
                    act.wait_ge(S["negmax_ready"], i + 1)
                    ps = job_ps[JOBS.index(("energy", i)) % 2]
                    for n in (2 * i, 2 * i + 1):
                        ins = act.activation(att[:, n, :], ps[:, (n % 2) * T:(n % 2) * T + T], ACT.Exp,
                                             bias=smax[:, 0, n:n + 1], accum_out=smax[:, 1, n:n + 1])
                        if n % 2 == 0:
                            step(ins)
                    ins.then_inc(S["job_used"], 1)
                elif kind == "norm":
                    act.wait_ge(S["recip_ready"], 1)
                    for n in range(TILES):
                        act.activation(att[:, n, :], att[:, n, :], ACT.Copy, scale=smax[:, 2, n:n + 1])\
                           .then_inc(S["att_ready"], 1)
                elif kind == "attT":
                    i = item[1]
                    act.activation(attT[:, :, 2 * i:2 * i + 2, :], ps.rearrange("p (n k q) -> p k n q", n=2, k=2), ACT.Copy)\
                       .then_inc(S["job_used"], 1)
                elif kind in ("stat0", "stat1", "stat2"):
                    sqrt(int(kind[-1]), item[1], tiles_of(item[1]))
                elif kind == "rows0":
                    g = item[1]
                    normalize(0, g, tiles_of(g), lambda n: ztmp[:, n, :], lambda n: ps_tile(g, n))
                elif kind == "rows1":
                    g = item[1]
                    normalize(1, g, tiles_of(g), lambda n: x1[:, n, :], lambda n: ztmp[:, n, :])
                elif kind == "x1T":
                    g = item[1]
                    act.wait_ge(S["x1T_done"], g + 1)
                    act.activation(x1T, psA[g][:, :].rearrange("p (k t) -> p k t", k=2), ACT.Copy)\
                       .then_inc(S["x1T_ready"], 1)
                elif kind == "rows2":
                    g = item[1]
                    normalize(2, g, tiles_of(g), lambda n: x2[:, n, :], lambda n: ztmp[:, n, :])
                elif kind == "x2T":
                    g = item[1]
                    act.wait_ge(S["x2T_done"], g + 1)
                    act.activation(x2T16[:, 0, :, TB * g:TB * g + TB],
                                   psA[g][:, :].rearrange("p (k t) -> p k t", k=2), ACT.Copy, scale=X_UP)\
                       .then_inc(S["x2hi_ready"], 1)
                elif kind == "ffn":
                    g, n = item[1:]
                    s = NT * g + n
                    act.wait_ge(S["gate_done"], s + 1)
                    if s >= 2:
                        act.wait_ge(S["inter_ready"], s - 1)
                    act.activation(gelu[:, s % 2, :], gate_ps[s % 2], ACT.Gelu_apprx_tanh, scale=gm[:, 4, 0:1])\
                       .then_inc(S["gelu_done"], 1)
                    act.wait_ge(S["inter_ready"], s + 1)
                    act.activation(inter[g][:, 0, n, :], inter32[:, s % 2, :], ACT.Copy).then_inc(S["ihi_ready"], 1)
                elif kind == "out":
                    g = item[1]
                    for tiles in out_chunks(g):
                        sqrt(3, g, tiles)
                        normalize(3, g, tiles, lambda n: ztmp[:, n, :], lambda n: ff[:, n, :])

        @block.gpsimd
        def _(pool):
            steps = [0]

            def step(ins):
                steps[0] += 1
                ins.then_inc(pool_steps, 1)

            for item in PLAN:
                kind = item[0]
                if kind == "parts":
                    u = item[1]
                    if u == 0:
                        pool.wait_ge(S["decay_set"], 2)
                    if u:
                        pool.wait_ge(S["rest2_ready"], u)
                    pool.wait_ge(S["high_ready"], u + 1)
                    pool.tensor_tensor(rest[:, :], unit(V, u), vparts[:, u, 0, :], ALU.subtract).then_inc(S["rest1_ready"], 1)
                    pool.wait_ge(S["rest1_ready"], u + 1)
                    pool.wait_ge(S["mid_ready"], u + 1)
                    pool.tensor_tensor(vparts[:, u, 2, :], rest[:, :], vparts[:, u, 1, :], ALU.subtract)\
                        .then_inc(S["rest2_ready"], 1)
                elif kind == "G":
                    pool.wait_ge(S["absmax"], 1)
                    pool.partition_all_reduce(gm[:, 1, :], gm[:, 0, :], P, RMAX).then_inc(S["allmax"], 1)
                elif kind == "scan":
                    s = item[1]
                    q, j = SCANS[s]
                    pool.wait_ge(S["state_ready"], s + 1)
                    if s >= 4:
                        pool.wait_ge(S["sum_done"], s - 3)
                    if s == 3:
                        pool.wait_ge(S["absmax"], 1)
                    pool.tensor_tensor(prod[:, s % 4, :], state[:, s % 4, :], unit(R, q), ALU.mult)\
                        .then_inc(S["prod_ready"], 1)
                elif kind == "fin":
                    q = item[1]
                    pool.wait_ge(S["half_read"], q + 1)
                    pool.wait_ge(S["job_used"], used_jobs(unit_no(G, *PASSES[q])))
                    pool.tensor_tensor(og_cols(q), og_cols(q), unit(G, q), ALU.mult).then_inc(S["og_ready"], 1)
                elif kind == "piece":
                    d = item[1]
                    w, e, f = PIECES[d]
                    pool.wait_ge(S["scale_ready"], w + 1)
                    pool.wait_ge(S["bits_ready"], d + 1)
                    if d >= 2:
                        pool.wait_ge(S["lo_ready"], d - 1)
                    pool.tensor_tensor(full[:, d % 2, :], bits[:, 1 + d % 2, :].bitcast(F16),
                                       scales[:, w, PC * f:PC * f + PC], ALU.mult).then_inc(S["full_ready"], 1)
                elif kind == "aff0":
                    g = item[1]
                    pool.wait_ge(loaded["xtok"], 16)
                    pool.wait_ge(loaded["ln"], 16)
                    xg = xtok[:, GT * g:GT * g + GT, :]
                    pool.tensor_tensor(xg, xg, ln[:, 1:2, :].broadcast_to([P, GT, C]), ALU.add).then_inc(S["xlb_ready"], 1)
                elif kind == "aff":
                    g = item[1]
                    zg = ztmp[:, GT * g:GT * g + GT, :]
                    pool.wait_ge(S["normal_ready"], normals_before(0, g))
                    step(pool.tensor_tensor(zg, zg, ln[:, 0:1, :].broadcast_to([P, GT, C]), ALU.mult))
                    pool.wait_ge(pool_steps, steps[0])
                    pool.wait_ge(S["xlb_ready"], g + 1)
                    pool.tensor_tensor(zg, zg, xtok[:, GT * g:GT * g + GT, :], ALU.add).then_inc(S["z_ready"], 1)

        @block.tensor
        def _(pe):
            for item in PLAN:
                kind = item[0]
                if kind in ("proj", "qk", "energy", "attT"):
                    job = JOBS.index(item)
                    ps = job_ps[job % 2]
                    if job >= 2:
                        pe.wait_ge(S["job_used"], job - 1)
                if kind == "proj":
                    m, g, h = UNITS[item[1]]
                    i = MIXES.index((m, g))
                    pe.wait_ge(loaded[vp_weight(m)], 16)
                    pe.wait_ge(S["mix_ready"], i + 1)
                    for k in range(2):
                        mm = pe.matmul(ps, wproj[:, m, k, P * h:P * h + P], mix[:, i % 4, k, :], start=(k == 0), stop=(k == 1))
                    mm.then_inc(S["job_done"], 1)
                elif kind == "qk":
                    m, g = item[1] // 2, item[1] % 2
                    pe.wait_ge(loaded["ctx"], 16)
                    pe.wait_ge(loaded["wqk"], 16)
                    pe.matmul(ps, wqk[:, m, :], ctxT[:, TB * g:TB * g + TB], start=True, stop=True).then_inc(S["job_done"], 1)
                elif kind == "energy":
                    i = item[1]
                    pe.wait_ge(S["job_used"], JOBS.index(("qk", 3)) + 1)
                    for n in (2 * i, 2 * i + 1):
                        mm = pe.matmul(ps[:, (n % 2) * T:(n % 2) * T + T], queryT[:, P * n:P * n + P],
                                       keyT[:, T * (n // 2):T * (n // 2) + T], start=True, stop=True)
                    mm.then_inc(S["job_done"], 1)
                elif kind == "attT":
                    i = item[1]
                    pe.wait_ge(S["att_ready"], 2 * i + 2)
                    for n in range(2):
                        for k in range(2):
                            mm = pe.transpose(ps[:, (2 * n + k) * P:(2 * n + k + 1) * P], att[:, 2 * i + n, P * k:P * k + P],
                                              ident)
                    mm.then_inc(S["job_done"], 1)
                elif kind == "spread":
                    i = item[1]
                    q, j = SPREADS[i]
                    g, h = PASSES[q]
                    if i >= 2:
                        pe.wait_ge(S["spread_used"], i - 1)
                    if j is None:
                        pe.wait_ge(loaded["const"], 16)
                        pe.wait_ge(S["diag_ready"], q + 1)
                        mm = pe.matmul(spread_ps[i % 2], head_sum, diag, start=True, stop=True)
                    else:
                        if j % 4 == 0:
                            pe.wait_ge(stacked[q][j // 4], 48)
                        if j == 0:
                            pe.wait_ge(S["spread_w_ready"], 4)
                        mm = pe.matmul(spread_ps[i % 2], spread_w[:, j % 4, :], vstack[h][:, j // 4, TB * g:TB * g + TB],
                                       start=True, stop=True)
                    mm.then_inc(S["spread_done"], 1)
                elif kind == "sum":
                    s = item[1]
                    q, j = SCANS[s]
                    pe.wait_ge(S["prod_ready"], s + 1)
                    if j == 0 and q >= 2:
                        pe.wait_ge(S["half_read"], q - 1)
                    pe.matmul(sum_ps[q % 2], head_pick[:, 8 * (15 - j):8 * (15 - j) + P], prod[:, s % 4, :],
                              start=(j == 0), stop=(j == D - 1)).then_inc(S["sum_done"], 1)
                elif kind == "y":
                    g = item[1]
                    pe.wait_ge(loaded["wo"], 16)
                    pe.wait_ge(S["og_ready"], 2 * g + 2)
                    if g == 0:
                        pe.wait_ge(S["job_used"], len(JOBS))
                    for n in tiles_of(g):
                        for k in range(2):
                            mm = pe.matmul(ps_tile(g, n), og[:, k, P * n:P * n + P], wo[:, k, :], start=(k == 0), stop=(k == 1))
                    mm.then_inc(S["y_done"], 1)
                elif kind == "x1T":
                    g = item[1]
                    pe.wait_ge(S["normal_ready"], normals_before(1, g))
                    for k in range(2):
                        for n in tiles_of(g):
                            at = k * TB + (n % GT) * P
                            mm = pe.transpose(psA[g][:, at:at + P], x1[:, n, P * k:P * k + P], ident)
                    mm.then_inc(S["x1T_done"], 1)
                elif kind == "xm":
                    g = item[1]
                    pe.wait_ge(S["x1T_ready"], g + 1)
                    for n in tiles_of(g):
                        b = n * P // T
                        for k in range(2):
                            mm = pe.matmul(ps_tile(g, n), x1T[:, k, (n % GT) * P:(n % GT) * P + P],
                                           attT[:, k, 2 * b:2 * b + 2, :], start=(k == 0), stop=(k == 1))
                    mm.then_inc(S["xm_done"], 1)
                elif kind == "x2T":
                    g = item[1]
                    pe.wait_ge(S["normal_ready"], normals_before(2, g))
                    for k in range(2):
                        for n in tiles_of(g):
                            at = k * TB + (n % GT) * P
                            mm = pe.transpose(psA[g][:, at:at + P], x2[:, n, k:C:2], ident)
                    mm.then_inc(S["x2T_done"], 1)
                elif kind == "ffn":
                    g, n = item[1:]
                    s = NT * g + n
                    if n == 0:
                        pe.wait_ge(S["x2lo_ready"], g + 1)
                    if s == 0:
                        pe.wait_ge(S["lo_ready"], UPPIECES)
                        pe.wait_ge(S["spread_used"], len(SPREADS))
                    if s == 1:
                        pe.wait_ge(S["half_read"], len(PASSES))
                    for w, ps, done, used in ((0, gate_ps, "gate_done", "gelu_done"), (1, up_ps, "up_done", "inter_ready")):
                        if s >= 2:
                            pe.wait_ge(S[used], s - 1)
                        passes = [(k, a, b) for k in range(2) for a, b in ((0, 0), (0, 1), (1, 0))]
                        for i, (k, a, b) in enumerate(passes):
                            mm = pe.matmul(ps[s % 2], w16[:, w, k, a, n * P:n * P + P], x2T16[:, b, k, TB * g:TB * g + TB],
                                           start=(i == 0), stop=(i == 5))
                        mm.then_inc(S[done], 1)
                elif kind == "down":
                    g = item[1]
                    pe.wait_ge(S["ilo_ready"], NT * (g + 1))
                    pe.wait_ge(S["lo_ready"], len(PIECES))
                    if g:
                        pe.wait_ge(S["var_ready"], norm_no(3, 0) + 1)
                    for n in tiles_of(g):
                        at = (n % GT) * P
                        passes = [(m, a, b) for m in range(NT) for a, b in ((0, 0), (0, 1), (1, 0))]
                        for i, (m, a, b) in enumerate(passes):
                            mm = pe.matmul(down_tile(g, n), inter[g][:, a, m, at:at + P],
                                           w16[:, 2, m % 2, b, (m // 2) * C:(m // 2) * C + C],
                                           start=(i == 0), stop=(i == len(passes) - 1))
                        mm.then_inc(S["down_done"], 1)

        @block.vector
        def _(dve):
            steps = [0]

            def step(ins):
                steps[0] += 1
                ins.then_inc(vec, 1)

            def own():
                dve.wait_ge(vec, steps[0])

            def stats(i, g, tiles, src):
                for n in tiles:
                    step(dve.bn_stats(lnst[:, n % 2, :], src(n)))
                    own()
                    ins = dve.bn_aggr(mv[:, i, n, :], lnst[:, n % 2, :])
                    if n != tiles[-1]:
                        step(ins)
                ins.then_inc(S["var_ready"], 1)

            def rows(i, g, tiles):
                a, b = tiles[0], tiles[-1] + 1
                dve.wait_ge(S["sqrt_done"], norm_no(i, g, tiles) + 1)
                step(dve.reciprocal(rstd[:, i, a:b], rstd[:, i, a:b]))
                own()
                dve.wait_ge(S["var_ready"], norm_no(i, g, tiles) + 1)
                dve.scalar_tensor_tensor(out=shift[:, i, a:b], in0=mv[:, i, a:b, 0], scalar=-1.0, in1=rstd[:, i, a:b],
                                         op0=ALU.mult, op1=ALU.mult).then_inc(S["rows_ready"], 1)

            kvb = [kv[:, s, :].rearrange("p (b t) -> p b t", t=T) for s in range(2)]
            step(dve.memset(keep[:, :], 1.0))
            own()
            step(dve.memset(keep[:, 0:TB:T], 0.0))
            step(dve.memset(eps[:, :], EPS))
            for s in range(2):
                step(dve.memset(kvb[s][:, :, 0:1], 0.0))

            for item in PLAN:
                kind = item[0]
                if kind == "xx":
                    g = item[1]
                    dve.wait_ge(loaded[f"x{g}"], 16)
                    xb = xT[:, :, TB * g:TB * g + TB].rearrange("p h (b t) -> p h b t", t=T)
                    xxb = xx[:, :, TB * g:TB * g + TB].rearrange("p h (b t) -> p h b t", t=T)
                    step(dve.tensor_tensor(xxb[:, :, :, 1:T], xb[:, :, :, 0:T - 1], xb[:, :, :, 1:T], ALU.subtract))
                    step(dve.tensor_tensor(xxb[:, :, :, 0:1], xb[:, :, :, 1:2], xb[:, :, :, 0:1], ALU.subtract))
                    xx_at = steps[0]
                elif kind == "mix":
                    i = item[1]
                    m, g = MIXES[i]
                    dve.wait_ge(vec, xx_at)
                    if i == 0:
                        dve.wait_ge(loaded["cvec"], 16)
                    if i >= 4:
                        dve.wait_ge(S["job_done"], used_jobs(unit_no(m, 0, 1)))
                    for h in range(2):
                        ins = dve.scalar_tensor_tensor(out=mix[:, i % 4, h, :], in0=xx[:, h, TB * g:TB * g + TB],
                                                       scalar=cvec[:, h, m:m + 1], in1=xT[:, h, TB * g:TB * g + TB],
                                                       op0=ALU.mult, op1=ALU.add)
                    ins.then_inc(S["mix_ready"], 1)
                    if i == 2:
                        dve.wait_ge(loaded["const"], 16)
                        for j in range(4):
                            dve.tensor_scalar(spread_w[:, j, :], head_spread[0:96, :], lane[0:96, j:j + 1], None, ALU.mult)\
                               .then_inc(S["spread_w_ready"], 1)
                elif kind == "diag":
                    q = item[1]
                    g, h = PASSES[q]
                    dve.wait_ge(S["job_used"], used_jobs(unit_no(R, g, h)))
                    if q:
                        dve.wait_ge(S["spread_done"], SPREADS.index((q - 1, None)) + 1)
                    dve.scalar_tensor_tensor(out=diag, in0=unit(K, q), scalar=cvec[:, h, 5:6], in1=unit(R, q),
                                             op0=ALU.mult, op1=ALU.mult).then_inc(S["diag_ready"], 1)
                elif kind == "use":
                    i = item[1]
                    q, j = SPREADS[i]
                    dve.wait_ge(S["spread_done"], i + 1)
                    if j is None:
                        if q:
                            dve.wait_ge(S["rest2_ready"], q + 1)
                        dve.tensor_tensor(og_cols(q), spread_ps[i % 2], unit(V, q), ALU.mult).then_inc(S["spread_used"], 1)
                    else:
                        s = SCANS.index((q, j))
                        if s >= 2:
                            dve.wait_ge(S["state_ready"], s - 1)
                        vb = spread_ps[i % 2].rearrange("p (b t) -> p b t", t=T)
                        kb = unit(K, q).rearrange("p (b t) -> p b t", t=T)
                        dve.tensor_tensor(kvb[s % 2][:, :, 1:T], vb[:, :, 0:T - 1], kb[:, :, 0:T - 1], ALU.mult)\
                           .then_inc(S["spread_used"], 1)
                elif kind == "scan":
                    s = item[1]
                    q, j = SCANS[s]
                    h = PASSES[q][1]
                    dve.wait_ge(S["spread_used"], SPREADS.index((q, j)) + 1)
                    if s == 0:
                        dve.wait_ge(S["decay_set"], 2)
                        own()
                    if s >= 4:
                        dve.wait_ge(S["prod_ready"], s - 3)
                    dve.tensor_tensor_scan(state[:, s % 4, :], decay_ps[:, TB * h:TB * h + TB], kv[:, s % 2, :], 0.0,
                                           ALU.mult, ALU.add).then_inc(S["state_ready"], 1)
                    if s == 1:
                        dve.wait_ge(loaded["flat"], 16)
                        dve.tensor_reduce(gm[:, 0, :], flat, AX.X, ALU.max, apply_absolute_value=True)\
                           .then_inc(S["absmax"], 1)
                elif kind == "fin":
                    q = item[1]
                    dve.wait_ge(S["sum_done"], D * (q + 1))
                    dve.wait_ge(S["spread_used"], SPREADS.index((q, None)) + 1)
                    dve.tensor_tensor(og_cols(q), sum_ps[q % 2], og_cols(q), ALU.add).then_inc(S["half_read"], 1)
                elif kind == "G":
                    dve.wait_ge(S["allmax"], 1)
                    step(dve.tensor_scalar(gm[:, 1, :], gm[:, 1, :], 2.0 ** -60, None, ALU.max))
                    own()
                    step(dve.tensor_scalar(gm[:, 2, :].bitcast(I32), gm[:, 1, :].bitcast(I32), 0x7F800000, None,
                                           ALU.bitwise_and))
                    own()
                    step(dve.reciprocal(gm[:, 5, :], gm[:, 2, :]))
                    own()
                    dve.tensor_scalar(gm[:, 3, :], gm[:, 5, :], W_UP * CODE_UP, None, ALU.mult).then_inc(S["g_ready"], 1)
                    step(dve.tensor_scalar(gm[:, 4, 0:1], gm[:, 2, 0:1], 1.0 / (X_UP * W_UP), None, ALU.mult))
                    step(dve.tensor_scalar(gm[:, 4, 1:2], gm[:, 5, 0:1], I_DOWN / (X_UP * W_UP), None, ALU.mult))
                    step(dve.tensor_tensor(gm[:, 6, 0:1], gm[:, 2, 0:1], gm[:, 2, 1:2], ALU.mult))
                    own()
                    step(dve.tensor_scalar(gm[:, 4, 2:3], gm[:, 6, 0:1], gm[:, 2, 2:3], 1.0 / (I_DOWN * W_UP),
                                           ALU.mult, ALU.mult))
                elif kind == "piece":
                    d = item[1]
                    w, e, f = PIECES[d]
                    dve.wait_ge(S["codes_ready"], w + 1)
                    if d == 0:
                        dve.wait_ge(S["mix_ready"], len(MIXES))
                    else:
                        dve.wait_ge(S["bits_ready"], d)
                    if d >= 2:
                        dve.wait_ge(S["full_ready"], d - 1)
                    src = p16[:, w, PC * f:PC * f + PC].bitcast(U32)
                    magnitude, code = bits[:, 0, :].bitcast(U32), bits[:, 1 + d % 2, :].bitcast(U32)
                    step(dve.tensor_scalar(magnitude, src, 9 - 4 * e, 0x0E000E00, ALU.logical_shift_left, ALU.bitwise_and))
                    step(dve.tensor_scalar(code, src, 12 - 4 * e, 0x80008000, ALU.logical_shift_left, ALU.bitwise_and))
                    own()
                    dve.tensor_tensor(code, code, magnitude, ALU.bitwise_or).then_inc(S["bits_ready"], 1)
                elif kind == "low":
                    d = item[1]
                    w, e, f = PIECES[d]
                    cols = slice(PC * f, PC * f + PC)
                    dve.wait_ge(S["hi_ready"], d + 1)
                    dve.tensor_tensor(w16[:, w, e, 1, cols], full[:, d % 2, :], w16[:, w, e, 0, cols], ALU.subtract)\
                       .then_inc(S["lo_ready"], 1)
                elif kind == "energy":
                    i = item[1]
                    job = JOBS.index(item)
                    dve.wait_ge(S["job_done"], job + 1)
                    dve.tensor_reduce(smax[:, 0, 2 * i:2 * i + 2], job_ps[job % 2].rearrange("p (n k) -> p n k", n=2),
                                      AX.X, ALU.max, negate=True).then_inc(S["negmax_ready"], 1)
                elif kind == "rowsum":
                    dve.wait_ge(S["job_used"], JOBS.index(("energy", 3)) + 1)
                    dve.reciprocal(smax[:, 2, :], smax[:, 1, :]).then_inc(S["recip_ready"], 1)
                elif kind == "stat0":
                    g = item[1]
                    dve.wait_ge(S["y_done"], g + 1)
                    stats(0, g, tiles_of(g), lambda n: ps_tile(g, n))
                elif kind == "stat1":
                    g = item[1]
                    dve.wait_ge(S["z_ready"], g + 1)
                    stats(1, g, tiles_of(g), lambda n: ztmp[:, n, :])
                elif kind in ("rows0", "rows1", "rows2"):
                    rows(int(kind[-1]), item[1], tiles_of(item[1]))
                elif kind == "stat2":
                    g = item[1]
                    dve.wait_ge(S["xm_done"], g + 1)
                    zg = ztmp[:, GT * g:GT * g + GT, :]
                    step(dve.tensor_tensor(zg, psA[g][:, :].rearrange("p (n c) -> p n c", n=GT),
                                           x1[:, GT * g:GT * g + GT, :], ALU.add))
                    own()
                    stats(2, g, tiles_of(g), lambda n: ztmp[:, n, :])
                elif kind == "x2lo":
                    g = item[1]
                    dve.wait_ge(S["x2hi_ready"], g + 1)
                    dve.scalar_tensor_tensor(out=x2T16[:, 1, :, TB * g:TB * g + TB],
                                             in0=psA[g][:, :].rearrange("p (k t) -> p k t", k=2), scalar=X_UP,
                                             in1=x2T16[:, 0, :, TB * g:TB * g + TB], op0=ALU.mult, op1=ALU.subtract)\
                       .then_inc(S["x2lo_ready"], 1)
                elif kind == "ffn":
                    g, n = item[1:]
                    s = NT * g + n
                    dve.wait_ge(S["gelu_done"], s + 1)
                    dve.wait_ge(S["up_done"], s + 1)
                    if s >= 2:
                        dve.wait_ge(S["ilo_ready"], s - 1)
                    dve.scalar_tensor_tensor(out=inter32[:, s % 2, :], in0=up_ps[s % 2], scalar=gm[:, 4, 1:2],
                                             in1=gelu[:, s % 2, :], op0=ALU.mult, op1=ALU.mult).then_inc(S["inter_ready"], 1)
                    if s == 0:
                        dve.wait_ge(S["og_ready"], len(PASSES))
                    if s == NT // 2:
                        dve.wait_ge(S["y_done"], 2)
                    dve.wait_ge(S["ihi_ready"], s + 1)
                    dve.tensor_tensor(inter[g][:, 1, n, :], inter32[:, s % 2, :], inter[g][:, 0, n, :], ALU.subtract)\
                       .then_inc(S["ilo_ready"], 1)
                elif kind == "out":
                    g = item[1]
                    done = GT * g
                    for tiles in out_chunks(g):
                        a, b = tiles[0], tiles[-1] + 1
                        done += len(tiles)
                        dve.wait_ge(S["down_done"], done)
                        dve.wait_ge(S["normal_ready"], normals_before(2, g))
                        step(dve.scalar_tensor_tensor(
                            out=ff[:, a:b, :].rearrange("p n c -> p (n c)"),
                            in0=psA[0][:, :] if g == 0 else down_tile(g, a), scalar=gm[:, 4, 2:3],
                            in1=x2[:, a:b, :].rearrange("p n c -> p (n c)"), op0=ALU.mult, op1=ALU.add))
                        own()
                        stats(3, g, tiles, lambda n: ff[:, n, :])
                        rows(3, g, tiles)


def kernel(**inputs):
    import numpy as np
    import concourse.bacc as bacc
    from concourse.bass_utils import run_bass_kernel_spmd

    a = {k: np.asarray(v) for k, v in inputs.items()}
    n, c = N, C

    def hidden_order(w):
        return w.reshape(w.shape[0], 8, P, 2).transpose(0, 1, 3, 2).reshape(w.shape[0], MLP)

    def dim_major(w):
        return w.reshape(2, HPH, D, -1).transpose(0, 2, 1, 3).reshape(c, -1)

    x = a["x"].reshape(n, c)
    gate, up, down = (a[f"L0_ffn_{m}_W_packed"] for m in ("gate", "up", "down"))
    sg, su, sd = (a[f"L0_ffn_{m}_scales"] for m in ("gate", "up", "down"))
    lanes = np.arange(P)
    to_sum = (lanes[:, None] // D == lanes[None, :] % HPH).astype(np.float32)
    pick = np.zeros((P, 248), np.float32)
    pick[lanes, 120 + lanes // D] = 1.0
    consts = np.concatenate([np.eye(P, dtype=np.float32), to_sum, pick, to_sum.T,
                             (lanes[:, None] // HPH % 4 == np.arange(4)[None, :]).astype(np.float32)], axis=1)
    data = {
        "x_chan": x.T,
        "x_tok": x,
        "ctx_chan": a["ctx_1024"].reshape(n, P).T,
        "w_chan": np.stack([dim_major(a["L0_attn_Wv"]).T, a["L0_attn_Wk"].T, a["L0_attn_Wr"].T,
                            dim_major(a["L0_attn_Wg"]).T, dim_major(a["L0_attn_Wo"].T)]),
        "chan_vecs": np.stack([a["L0_attn_tm_" + m] for m in "vkrg"] + [a["L0_attn_time_decay"].reshape(c),
                              a["L0_attn_time_first"].reshape(c)], axis=1),
        "ln_vecs": np.stack([a["L0_attn_ln_w"], a["L0_attn_ln_b"]]),
        "xq_chan": np.stack([a["L0_xattn_Wq"].T, a["L0_xattn_Wk"].T]),
        "xq_bias": np.stack([a["L0_xattn_bq"], a["L0_xattn_bk"]], axis=1),
        "packed": np.stack([hidden_order(gate.T), hidden_order(up.T),
                            down.T.reshape(8, P, c).transpose(1, 0, 2).reshape(P, MLP)]),
        "scale_rows_in": np.stack([hidden_order(sg.T), hidden_order(su.T)]),
        "scale_rows_out": sd.T.reshape(8, 8, c),
        "scale_flat": np.stack([sg.reshape(-1), su.reshape(-1), sd.reshape(-1)]),
        "consts": consts,
    }
    nc = bacc.Bacc("TRN2", target_bir_lowering=False, num_devices=1)
    arrays, args = {}, []
    for name, value in data.items():
        value = np.ascontiguousarray(value)
        arrays[name] = value
        args.append(nc.dram_tensor(name, value.shape, mybir.dt.from_np(value.dtype), kind="ExternalInput").ap())
    args.append(nc.dram_tensor("out", (n, c), F32, kind="ExternalOutput").ap())
    decoder_layer(nc, *args)
    result = run_bass_kernel_spmd(nc, [arrays], core_ids=[0])
    return result.results[0]["out"].reshape(B, T, C)
```

```python
from contextlib import ExitStack

import concourse.bass as bass
from concourse import mybir

ALU = mybir.AluOpType
ACT = mybir.ActivationFunctionType
F32 = mybir.dt.float32
F16 = mybir.dt.float16
BF16 = mybir.dt.bfloat16
I32 = mybir.dt.int32
U32 = mybir.dt.uint32
U16 = mybir.dt.uint16
AX = mybir.AxisListType
RMAX = bass.bass_isa.ReduceOp.max

P = 128
B, T, C = 4, 256, 256
N = B * T
D = 16
HPH = P // D
GROUPS = 2
TB = N // GROUPS
GT = TB // P
TILES = N // P
MLP = 2048
NT = MLP // P
PC = 512
EPS = 1e-5
X_UP = 2048.0
W_UP = 4096.0
I_DOWN = 2.0 ** -8
CODE_UP = 2.0 ** 14

V, K, R, G = range(4)
SLOT = {K: 0, R: 1, G: 2, V: 3}
UNITS = [(V, 0, 0), (K, 0, 0), (R, 0, 0), (V, 0, 1), (K, 0, 1), (R, 0, 1), (G, 0, 0), (G, 0, 1)]
UNITS += [(m, 1, h) for m in (V, K, R, G) for h in range(2)]
MIXES = [(m, g) for g in range(GROUPS) for m in (V, K, R, G)]
PASSES = [(g, h) for g in range(GROUPS) for h in range(2)]
SCANS = [(q, j) for q in range(len(PASSES)) for j in range(D)]
STATES, PRODS = 4, 5
FIRST = 4
SPREADS = [(0, j) for j in (*range(6), None, *range(6, D))]
SPREADS += [(q, j) for q in range(1, len(PASSES)) for j in (None, *range(D))]
QUARTERS = range(2048 // PC)
PIECES = [(w, e, f) for w in (0, 1) for f in (0, 1) for e in range(2)]
PIECES += [(w, e, f) for f in (2, 3) for w in (0, 1) for e in range(2)]
PIECES += [(2, e, f) for f in QUARTERS for e in range(2)]
POOL_LOW = 8


STEP_OF = {
    "G": {(): 8},
    "aff": {(0, 0): 40.6, (0, 1): 43.4, (1, 0): 67.4, (1, 1): 69.4},
    "aff0": {(0, 0): 32.6, (0, 1): 36.6, (1, 0): 59.0, (1, 1): 59.8},
    "attT": {0: 32.1, 1: 33.1, 2: 34.5, 3: 35.5},
    "codes": {0: 4.8, 1: 7.8, 2: 15.8},
    "diag": {0: 2.8},
    "down": {0: 79.6, 1: 101.8},
    "energy": {0: 26.2, 1: 27.4, 2: 28, 3: 29},
    "exp": {0: 28.5, 1: 29.3, 2: 29.7, 3: 31.1},
    "flat": {(): 1.4},
    "high": {0: -3.4, 1: 0.6, 2: 11.0, 3: 16.8},
    "low": {0: 17.4, 1: 17.8, 2: 19.0, 3: 22.9, 4: 28.6, 5: 33.3, 6: 34.5, 7: 34.8, 8: 64.9, 9: 65.0, 10: 66.2,
            11: 67.2, 12: 68.2, 13: 69.0, 14: 69.6, 15: 70.6, 16: 70.8, 17: 72.2, 18: 72.2, 19: 73.4, 20: 74.2,
            21: 75.2, 22: 76.2, 23: 80.0},
    "mid": {0: 0, 1: 3, 2: 15.4, 3: 19.0},
    "mix": {3: -1, 4: 2, 5: 3, 6: 3.6, 7: 11},
    "norm": {(): 31.4},
    "out": {0: 82.6, 1: 96.6},
    "piece": {0: 13.6, 1: 15.2, 2: 17.4, 3: 19.4, 4: 24.0, 5: 28.5, 6: 30.4, 7: 32.5, 8: 63.2, 9: 63.4, 10: 65.0,
            11: 65.4, 12: 66.2, 13: 67.0, 14: 67.8, 15: 68.6, 16: 69.4, 17: 70.2, 18: 71.2, 19: 71.8, 20: 72.4,
            21: 73.0, 22: 74.0, 23: 74.8},
    "proj": {3: 0, 4: 0.8, 5: 1, 6: 2.8, 7: 6.4, 8: 10, 9: 15.4, 10: 16.0, 11: 16.2, 12: 18.4, 13: 20.0, 14: 22.4,
            15: 25},
    "qk": {0: 19.4, 1: 21.4, 2: 23.4, 3: 24},
    "rows0": {0: 40.6, 1: 67},
    "rows1": {0: 47, 1: 72},
    "rows2": {0: 57.6, 1: 78.1},
    "rowsum": {(): 31.0},
    "scale": {0: 11.0, 1: 12.2, 2: 62},
    "spread_w": {(): 1.0},
    "stat0": {0: 38.9, 1: 66},
    "stat1": {0: 45.6, 1: 70.6},
    "stat2": {0: 54.6, 1: 76.7},
    "x1T": {0: 51.4, 1: 74.6},
    "x2T": {0: 59.0, 1: 79.1},
    "x2lo": {0: 59.6, 1: 79.8},
    "xm": {0: 53.2, 1: 75.6},
    "xx": {1: -2},
    "y": {0: 37.0, 1: 64.6},
}
BESIDE = {(kind, *(index if isinstance(index, tuple) else (index,))): step
          for kind, steps in STEP_OF.items() for index, step in steps.items()}
LAG = {
    ("act", "attT"): 1, ("act", "codes"): -0.3, ("act", "piece"): 1.6, ("act", "proj"): 0.2, ("act", "rows1"): 1,
    ("act", "rows2"): -0.6, ("act", "split"): 0.7, ("act", "stat0"): 0.6, ("act", "x1T"): -0.6, ("act", "x2T"):
    -0.3, ("pool", "high"): 1, ("pool", "mid"): 1, ("pool", "piece"): 0.7, ("tensor", "energy"): -1, ("tensor",
    "sum"): 1, ("tensor", "x2T"): -0.6, ("vector", "G"): 0.6, ("vector", "down"): 0.3, ("vector", "energy"): 0.4,
    ("vector", "rows1"): -0.6, ("vector", "rows2"): -1, ("vector", "split"): 1, ("vector", "spread_w"): -0.6,
    ("vector", "stat2"): -0.3, ("vector", "use"): 0.6, ("act", "ffn", 1, 3): -1, ("act", "proj", 0): -1.9, ("act",
    "split", 0, 3): -0.3, ("act", "split", 0, 14): 0.6, ("pool", "scan", 1): 1, ("tensor", "spread", 41): 0.6,
    ("tensor", "sum", 44): 0.1, ("tensor", "x1T", 1): 1, ("vector", "ffn", 1, 3): -0.3, ("vector", "scan", 29):
    -0.3, ("vector", "split", 0, 12): 0.6, ("vector", "split", 1, 15): -1, ("vector", "stat2", 0): 0.3
}


def make_plan():
    plan = [(-2, item) for item in (("xx", 0), ("mix", 0), ("mix", 1), ("first_w",), ("proj", 0), ("proj", 1),
                                    ("spread", 0), ("spread", 1), ("mix", 2), ("proj", 2), ("use", 0), ("spread", 2), ("use", 1))]
    for s, (q, j) in enumerate(SCANS):
        here = SPREADS.index((q, j))
        upto = SPREADS.index(SCANS[s + 1]) if s + 1 < len(SCANS) else here
        for i in range(here + 1, upto + 1):
            if i + 1 < len(SPREADS) and i > 1:
                plan.append((s, ("spread", i + 1)))
            if i > 1:
                plan.append((s, ("use", i)))
        plan += [(s, ("scan", s)), (min(s + 1, len(SCANS) - 1.2), ("sum", s))]
        if j == 3 and q:
            plan.append((s, ("fin", q - 1)))
        if j == 8 and q + 1 < len(PASSES):
            plan.append((s, ("diag", q + 1)))
    plan.append((len(SCANS) - 1, ("fin", len(PASSES) - 1)))
    for g in range(GROUPS):
        for n in range(NT):
            t = len(SCANS) + (NT + 1) * g + n
            plan += [(t if (g, n) != (0, 0) else len(SCANS) - 1.5, ("hidden", g, n)), (t, ("ffn", g, n)), (t, ("split", g, n))]
    plan += [(t + 0.5, item) for item, t in BESIDE.items()]
    return sorted(plan, key=lambda entry: entry[0])


TIMED_PLAN = make_plan()
PLAN = [item for _, item in TIMED_PLAN]


def plan_of(engine):
    timed = [(t + LAG.get((engine, item[0]), 0) + LAG.get((engine, *item), 0), item) for t, item in TIMED_PLAN]
    mine = [item for _, item in sorted(timed, key=lambda entry: entry[0])]
    for kind in {item[0] for item in PLAN}:
        assert [i for i in mine if i[0] == kind] == [i for i in PLAN if i[0] == kind]
    return mine


JOBS = [item for item in PLAN if item[0] in ("proj", "qk", "energy", "attT")]


def decoder_layer(nc, x_chan, x_tok, ctx_chan, w_chan, chan_vecs, ln_vecs, xq_chan, xq_bias,
                  packed, scale_rows_in, scale_rows_out, scale_flat, consts, out):
    with ExitStack() as stack:
        def sb(name, shape, dt=F32):
            return stack.enter_context(nc.sbuf_tensor(name, shape, dt))

        def sem(name):
            return stack.enter_context(nc.semaphore(name))

        region_a = sb("region_a", [P, 8192])
        xT = region_a[:, 0:2048].rearrange("p (h t) -> p h t", h=2)
        xx = region_a[:, 2048:4096].rearrange("p (h t) -> p h t", h=2)
        mix = region_a[:, 4096:8192].rearrange("p (m h t) -> p m h t", m=4, h=2)
        bits = region_a[:, 0:768].bitcast(U16).rearrange("p (s n) -> p s n", s=3)
        full = region_a[:, 1024:2048].rearrange("p (s n) -> p s n", s=2)
        xtok = region_a[:, 6144:8192].rearrange("p (n c) -> p n c", n=TILES)
        region_b = sb("region_b", [P, 8192])
        proj = region_b[:, :].rearrange("p (m h t) -> p m h t", m=4, h=2)
        og = proj[:, SLOT[V]]
        inter = [r[:, :].bitcast(F16).rearrange("p (m n t) -> p m n t", m=2, n=NT) for r in (region_b, region_a)]
        region_c = sb("region_c", [P, 8704])
        kv = region_c[:, 0:1024].rearrange("p (s t) -> p s t", s=2)
        state = region_c[:, 1024:3072].rearrange("p (s t) -> p s t", s=STATES)
        prod = region_c[:, 3072:5632].rearrange("p (s t) -> p s t", s=PRODS)
        flat = region_c[:, 7936:8320].rearrange("p (w n) -> p w n", w=3)
        vparts = region_c[:, 5632:8704].bitcast(BF16).rearrange("p (u m t) -> p u m t", u=4, m=3)
        ztmp = region_c[:, 5632:7680].rearrange("p (n c) -> p n c", n=TILES)
        x1T = region_c[:, 7680:8704].rearrange("p (k t) -> p k t", k=2)
        gelu = region_c[:, 0:1024].rearrange("p (s t) -> p s t", s=2)
        inter32 = region_c[:, 1024:2048].rearrange("p (s t) -> p s t", s=2)
        ff = region_c[:, 2048:4096].rearrange("p (n c) -> p n c", n=TILES)

        w16 = sb("w16", [P, 3, 2, 2, 2048], F16)
        wproj = w16[:, 1, 0].rearrange("p m n -> p (m n)").bitcast(F32).rearrange("p (m k n) -> p m k n", m=4, k=2)
        packed_in = w16[:, 0].rearrange("p e m n -> p (e m n)").bitcast(I32).rearrange("p (w n) -> p w n", w=2)
        packed_down = w16[:, 1, 1].rearrange("p m n -> p (m n)").bitcast(I32)
        early = w16[:, 2].rearrange("p e m n -> p (e m n)").bitcast(F32)
        ctxT = early[:, 0:1024]
        queryT = early[:, 1024:2048]
        keyT = early[:, 2048:3072]
        first_w = queryT[:, 0:FIRST * P].rearrange("p (j n) -> p j n", j=FIRST)
        wqk = early[:, 3072:3328].rearrange("p (m n) -> p m n", m=2)
        diag = early[:, 3328:3840]
        p16 = sb("p16", [P, 3, 2048], U16)
        scales = sb("scales", [P, 3, 2048])
        x1 = scales[:, 0, :].rearrange("p (n c) -> p n c", n=TILES)
        x2 = scales[:, 1, :].rearrange("p (n c) -> p n c", n=TILES)
        att = scales[:, 2, :].rearrange("p (n k) -> p n k", n=TILES)
        x2T16 = p16[:, 0:2, :].bitcast(F16).rearrange("p m (g k t) -> p m g k t", g=GROUPS, k=2)
        attT = sb("attT", [P, 2, TILES, P])
        vstack = [sb("vstack0", [96, 4, N], BF16),
                  region_a[0:96, 2048:4096].bitcast(BF16).rearrange("p (q t) -> p q t", q=4)]
        const = sb("const", [P, 504])
        ident = const[:, 0:128]
        head_sum = const[:, 128:256]
        head_pick = const[:, 256:504]
        head_spread = early[:, 3840:3968]
        qkb = early[:, 3976:3978]
        smax = early[:, 3984:4008].rearrange("p (k n) -> p k n", k=3)
        lane = early[:, 3968:3976]
        spread_w = sb("spread_w", [96, 4, P], BF16)
        keep = sb("keep", [P, TB])
        rest = keep
        wo = sb("wo", [P, 2, C])
        ln = sb("ln", [P, 2, C])
        cvec = sb("cvec", [P, 2, 6])
        decay = sb("decay", [P, 2, 2])
        gm = sb("gm", [P, 8, 3])
        lnst = sb("lnst", [P, GT, 6])
        mv = sb("mv", [P, 4, TILES, 2])
        rstd = sb("rstd", [P, 4, TILES])
        shift = sb("shift", [P, 4, TILES])
        eps = sb("eps", [P, 1])

        psA = [stack.enter_context(nc.psum_tensor(f"psA{i}", [P, 1024], F32)) for i in range(2)]
        psB = stack.enter_context(nc.psum_tensor("psB", [P, 4, TB], F32))
        job_ps = [psA[0][:, 0:TB], psA[0][:, TB:1024]]
        spread_ps = [psB[:, 0, :], psB[:, 1, :]]
        sum_ps = [psB[:, 2, :], psB[:, 3, :]]
        gate_ps = [psB[:, 0, :], psB[:, 2, :]]
        up_ps = [psB[:, 1, :], psB[:, 3, :]]
        decay_ps = psA[1]

        loads = ["x0_half0", "x0_half1", "x1_half0", "x1_half1", "cvec", "wv", "wk", "wr", "wg", "spreads", "const",
                 "ctx", "wqk", "qkb", "packed_in", "packed_down", "flat", "scales_in", "scales_out", "wo", "ln", "xtok"]
        loaded = {n: sem("loaded_" + n) for n in loads}
        stacked = [[sem(f"stacked{u}_{quad}") for quad in range(4)] for u in range(4)]
        vec = sem("vec_steps")
        act_steps = sem("act_steps")
        pool_steps = sem("pool_steps")
        names = """mix_ready job_done job_used decay_set spread_w_ready high_ready mid_ready rest1_ready rest2_ready
            diag_ready spread_done spread_used state_ready prod_ready sum_done half_read og_ready
            absmax allmax g_ready scale_ready codes_ready bits_ready full_ready hi_ready lo_ready
            negmax_ready recip_ready att_ready y_done var_ready sqrt_done rows_ready
            normal_ready xlb_ready z_ready x1T_done x1T_ready xm_done x2T_done x2hi_ready x2lo_ready
            gate_done up_done gelu_done inter_ready ihi_ready ilo_ready down_done stored""".split()
        S = {n: sem(n) for n in names}

        def vp_weight(m):
            return ("wv", "wk", "wr", "wg")[m]

        def unit_no(m, g, h):
            return UNITS.index((m, g, h))

        def used_jobs(u):
            return JOBS.index(("proj", u)) + 1

        def og_cols(q):
            g, h = PASSES[q]
            return og[:, h, TB * g:TB * g + TB]

        def unit(m, q):
            g, h = PASSES[q]
            return proj[:, SLOT[m], h, TB * g:TB * g + TB]

        def tiles_of(g):
            return list(range(GT * g, GT * g + GT))

        def pair_of(item):
            at = GT * item[1] + 2 * item[2]
            return slice(at, at + 2)

        def ps_tile(g, n):
            return psA[g][:, (n % GT) * C:(n % GT) * C + C]

        def low_part(engine, d):
            w, e, f = PIECES[d]
            cols = slice(PC * f, PC * f + PC)
            engine.wait_ge(S["hi_ready"], d + 1)
            if d == POOL_LOW:
                engine.wait_ge(S["lo_ready"], d)
            engine.tensor_tensor(w16[:, w, e, 1, cols], full[:, d % 2, :], w16[:, w, e, 0, cols], ALU.subtract)\
                  .then_inc(S["lo_ready"], 1)

        def pieces_for(quarter):
            return max(d for d, (w, _, f) in enumerate(PIECES) if w < 2 and f <= quarter) + 1

        def pieces_read(w, g):
            return max(d for d, (v, _, f) in enumerate(PIECES) if v == w and f // 2 <= g) + 1

        def hidden_ps(s):
            if s % 3 == 0:
                own_psA = psA[s // NT]
                return own_psA[:, 0:TB], own_psA[:, TB:1024]
            return gate_ps[s % 3 - 1], up_ps[s % 3 - 1]

        def down_tile(g, n):
            return ps_tile(g, n) if g == 0 else psA[n % GT // 2][:, n % 2 * TB:n % 2 * TB + C]

        def out_chunks(g):
            return [tiles_of(g)] if g == 0 else [[n] for n in tiles_of(g)]

        NORMS = []
        for item in PLAN:
            if item[0] in ("stat0", "stat1", "stat2"):
                NORMS.append((int(item[0][-1]), item[1], tiles_of(item[1])))
            elif item[0] == "out":
                NORMS += [(3, item[1], tiles) for tiles in out_chunks(item[1])]

        def norm_no(i, g, tiles=None):
            return NORMS.index((i, g, tiles or tiles_of(g)))

        def normals_before(i, g, tiles=None):
            return sum(len(t) for _, _, t in ACT_NORMS[:ACT_NORMS.index((i, g, tiles or tiles_of(g))) + 1])

        ACT_NORMS = []
        for item in PLAN:
            if item[0] in ("rows0", "rows1", "rows2"):
                ACT_NORMS.append((int(item[0][-1]), item[1], tiles_of(item[1])))
            elif item[0] == "out":
                ACT_NORMS += [(3, item[1], tiles) for tiles in out_chunks(item[1])]

        def normals(stage, tiles):
            return normals_before(3, stage[1], tiles)

        block = stack.enter_context(nc.Block())

        @block.sync
        def _(sp):
            def load(dst, src, name):
                sp.dma_start(dst, src).then_inc(loaded[name], 16)

            def load_x(g):
                for h in range(2):
                    load(xT[:, h, TB * g:TB * g + TB], x_chan[P * h:P * h + P, TB * g:TB * g + TB], f"x{g}_half{h}")

            def load_w(m):
                load(wproj[:, m], w_chan[m].rearrange("(k p) n -> p k n", p=P), vp_weight(m))

            def stack_v(u):
                g, h = PASSES[u]
                sp.wait_ge(S["rest2_ready"], u + 1)
                if u == 1:
                    sp.wait_ge(S["mix_ready"], 2 * len(MIXES))
                for quad in range(FIRST // 4 if u == 0 else 0, 4):
                    for m in range(3):
                        sp.dma_start(vstack[h][32 * m:32 * m + 32, quad, TB * g:TB * g + TB],
                                     vparts[32 * quad:32 * quad + 32, u, m, :]).then_inc(stacked[u][quad], 16)

            load_x(0)
            load(cvec[:, :, :], chan_vecs.rearrange("(h p) v -> p h v", p=P), "cvec")
            load_w(V)
            load_w(K)
            load(early[:, 3840:3976], consts[:, 504:640], "spreads")
            load_w(R)
            load(const[:, :], consts[:, 0:504], "const")
            load_x(1)
            load_w(G)
            load(flat, scale_flat.rearrange("w (p n) -> p w n", p=P), "flat")
            for w in range(2):
                load(packed_in[:, w, :], packed[w], "packed_in")
            stack_v(0)
            for k in range(8):
                load(scales[16 * k:16 * k + 16, 0:2, :],
                     scale_rows_in.rearrange("w k n -> k w n")[k:k + 1].broadcast_to([16, 2, 2048]), "scales_in")
            load(packed_down, packed[2], "packed_down")
            stack_v(1)
            load(ctxT, ctx_chan, "ctx")
            load(wqk, xq_chan.rearrange("m p n -> p m n"), "wqk")
            load(qkb, xq_bias, "qkb")
            load(wo[:, :, :], w_chan[4].rearrange("(k p) n -> p k n", p=P), "wo")
            load(ln[:, :, :], ln_vecs.partition_broadcast(P), "ln")
            stack_v(2)
            stack_v(3)
            sp.wait_ge(S["job_done"], used_jobs(len(UNITS) - 1))
            load(xtok, x_tok.rearrange("(n p) c -> p n c", p=P), "xtok")
            sp.wait_ge(S["job_used"], len(JOBS))
            for k in range(8):
                load(scales[16 * k:16 * k + 16, 2, :].rearrange("p (c n) -> p c n", c=8),
                     scale_rows_out[:, k, :].partition_broadcast(16), "scales_out")
            stores = 0
            for g in range(GROUPS):
                for tiles in out_chunks(g):
                    stores += 1
                    sp.wait_ge(S["normal_ready"], normals(("out", g), tiles))
                    sp.dma_start(out[P * tiles[0]:P * tiles[-1] + P].rearrange("(n p) c -> p n c", p=P),
                                 ztmp[:, tiles[0]:tiles[-1] + 1, :]).then_inc(S["stored"], 16)
            sp.wait_ge(S["stored"], 16 * stores)

        @block.scalar
        def _(act):
            steps = [0]

            def step(ins):
                steps[0] += 1
                ins.then_inc(act_steps, 1)

            def sqrt(i, g, tiles):
                act.wait_ge(S["var_ready"], norm_no(i, g, tiles) + 1)
                a, b = tiles[0], tiles[-1] + 1
                act.activation(rstd[:, i, a:b], mv[:, i, a:b, 1], ACT.Sqrt, bias=eps[:, 0:1]).then_inc(S["sqrt_done"], 1)

            def normalize(i, g, tiles, dst, src):
                act.wait_ge(S["rows_ready"], norm_no(i, g, tiles) + 1)
                for n in tiles:
                    act.activation(dst(n), src(n), ACT.Identity, bias=shift[:, i, n:n + 1], scale=rstd[:, i, n:n + 1])\
                       .then_inc(S["normal_ready"], 1)

            act.wait_ge(loaded["cvec"], 16)
            step(act.activation(decay[:, :, 0], cvec[:, :, 4], ACT.Exp))
            act.wait_ge(act_steps, steps[0])
            step(act.activation(decay[:, :, 1], decay[:, :, 0], ACT.Exp, scale=-1.0))
            act.wait_ge(act_steps, steps[0])
            act.wait_ge(vec, 3)
            for h in range(2):
                act.activation(decay_ps[:, TB * h:TB * h + TB], keep[:, :], ACT.Copy, scale=decay[:, h, 1:2])\
                   .then_inc(S["decay_set"], 1)

            for item in plan_of("act"):
                kind = item[0]
                if kind in ("proj", "qk", "attT"):
                    job = JOBS.index(item)
                    act.wait_ge(S["job_done"], job + 1)
                    ps = job_ps[job % 2]
                if kind == "proj":
                    m, g, h = UNITS[item[1]]
                    act.activation(proj[:, SLOT[m], h, TB * g:TB * g + TB], ps, ACT.Sigmoid if m == G else ACT.Copy)\
                       .then_inc(S["job_used"], 1)
                elif kind == "high":
                    u = item[1]
                    g, h = PASSES[u]
                    if u == 3:
                        act.wait_ge(S["absmax"], 1)
                    act.wait_ge(S["job_used"], used_jobs(unit_no(V, g, h)))
                    act.activation(vparts[:, u, 0, :], unit(V, u), ACT.Copy).then_inc(S["high_ready"], 1)
                elif kind == "mid":
                    u = item[1]
                    act.wait_ge(S["rest1_ready"], u + 1)
                    act.activation(vparts[:, u, 1, :], rest[:, :], ACT.Copy).then_inc(S["mid_ready"], 1)
                elif kind == "codes":
                    w = item[1]
                    act.wait_ge(loaded["packed_down" if w == 2 else "packed_in"], 16 if w == 2 else 32)
                    src = packed_down if w == 2 else packed_in[:, w, :]
                    act.activation(p16[:, w, :], src.bitcast(U16)[:, 0:4096:2], ACT.Copy).then_inc(S["codes_ready"], 1)
                elif kind == "scale":
                    w = item[1]
                    act.wait_ge(S["g_ready"], 1)
                    act.wait_ge(loaded["scales_out" if w == 2 else "scales_in"], 16 * 8)
                    act.activation(scales[:, w, :], scales[:, w, :], ACT.Copy, scale=gm[:, 3, w:w + 1])\
                       .then_inc(S["scale_ready"], 1)
                elif kind == "piece":
                    d = item[1]
                    w, e, f = PIECES[d]
                    act.wait_ge(S["full_ready"], d + 1)
                    if d == 0:
                        act.wait_ge(S["codes_ready"], 2)
                    if d == PIECES.index((1, 0, 0)):
                        act.wait_ge(S["job_done"], used_jobs(len(UNITS) - 1))
                        act.wait_ge(S["codes_ready"], 3)
                    act.activation(w16[:, w, e, 0, PC * f:PC * f + PC], full[:, d % 2, :], ACT.Copy)\
                       .then_inc(S["hi_ready"], 1)
                elif kind == "qk":
                    m, g = item[1] // 2, item[1] % 2
                    act.wait_ge(loaded["qkb"], 16)
                    act.activation((queryT, keyT)[m][:, TB * g:TB * g + TB], ps, ACT.Identity, bias=qkb[:, m:m + 1])\
                       .then_inc(S["job_used"], 1)
                elif kind == "exp":
                    i = item[1]
                    act.wait_ge(S["negmax_ready"], i + 1)
                    ps = job_ps[JOBS.index(("energy", i)) % 2]
                    for n in (2 * i, 2 * i + 1):
                        ins = act.activation(att[:, n, :], ps[:, (n % 2) * T:(n % 2) * T + T], ACT.Exp,
                                             bias=smax[:, 0, n:n + 1], accum_out=smax[:, 1, n:n + 1])
                        if n % 2 == 0:
                            step(ins)
                    ins.then_inc(S["job_used"], 1)
                elif kind == "norm":
                    act.wait_ge(S["recip_ready"], 1)
                    for n in range(TILES):
                        act.activation(att[:, n, :], att[:, n, :], ACT.Copy, scale=smax[:, 2, n:n + 1])\
                           .then_inc(S["att_ready"], 1)
                elif kind == "attT":
                    i = item[1]
                    act.activation(attT[:, :, 2 * i:2 * i + 2, :], ps.rearrange("p (n k q) -> p k n q", n=2, k=2), ACT.Copy)\
                       .then_inc(S["job_used"], 1)
                elif kind in ("stat0", "stat1", "stat2"):
                    sqrt(int(kind[-1]), item[1], tiles_of(item[1]))
                elif kind == "rows0":
                    g = item[1]
                    normalize(0, g, tiles_of(g), lambda n: ztmp[:, n, :], lambda n: ps_tile(g, n))
                elif kind == "rows1":
                    g = item[1]
                    act.wait_ge(S["full_ready"], pieces_read(0, g))
                    normalize(1, g, tiles_of(g), lambda n: x1[:, n, :], lambda n: ztmp[:, n, :])
                elif kind == "x1T":
                    g = item[1]
                    act.wait_ge(S["x1T_done"], g + 1)
                    act.activation(x1T, psA[g][:, :].rearrange("p (k t) -> p k t", k=2), ACT.Copy)\
                       .then_inc(S["x1T_ready"], 1)
                elif kind == "rows2":
                    g = item[1]
                    act.wait_ge(S["full_ready"], pieces_read(1, g))
                    normalize(2, g, tiles_of(g), lambda n: x2[:, n, :], lambda n: ztmp[:, n, :])
                elif kind == "x2T":
                    g = item[1]
                    act.wait_ge(S["x2T_done"], g + 1)
                    act.wait_ge(S["bits_ready"], pieces_read(1, g))
                    act.activation(x2T16[:, 0, g, :, :],
                                   psA[g][:, :].rearrange("p (k t) -> p k t", k=2), ACT.Copy, scale=X_UP)\
                       .then_inc(S["x2hi_ready"], 1)
                elif kind == "ffn":
                    g, n = item[1:]
                    s = NT * g + n
                    act.wait_ge(S["gate_done"], s + 1)
                    if s == 0:
                        act.wait_ge(S["state_ready"], len(SCANS))
                    if s >= 2:
                        act.wait_ge(S["inter_ready"], s - 1)
                    act.activation(gelu[:, s % 2, :], hidden_ps(s)[0], ACT.Gelu_apprx_tanh, scale=gm[:, 4, 0:1])\
                       .then_inc(S["gelu_done"], 1)
                elif kind == "split":
                    g, n = item[1:]
                    s = NT * g + n
                    act.wait_ge(S["inter_ready"], s + 1)
                    if s == 0:
                        act.wait_ge(S["og_ready"], len(PASSES))
                    act.activation(inter[g][:, 0, n, :], inter32[:, s % 2, :], ACT.Copy).then_inc(S["ihi_ready"], 1)
                elif kind == "out":
                    g = item[1]
                    for tiles in out_chunks(g):
                        sqrt(3, g, tiles)
                        normalize(3, g, tiles, lambda n: ztmp[:, n, :], lambda n: ff[:, n, :])

        @block.gpsimd
        def _(pool):
            steps = [0]

            def step(ins):
                steps[0] += 1
                ins.then_inc(pool_steps, 1)

            for item in plan_of("pool"):
                kind = item[0]
                if kind == "high":
                    u = item[1]
                    if u == 0:
                        pool.wait_ge(S["decay_set"], 2)
                    if u:
                        pool.wait_ge(S["rest2_ready"], u)
                    pool.wait_ge(S["high_ready"], u + 1)
                    pool.tensor_tensor(rest[:, :], unit(V, u), vparts[:, u, 0, :], ALU.subtract).then_inc(S["rest1_ready"], 1)
                elif kind == "mid":
                    u = item[1]
                    pool.wait_ge(S["rest1_ready"], u + 1)
                    pool.wait_ge(S["mid_ready"], u + 1)
                    pool.tensor_tensor(vparts[:, u, 2, :], rest[:, :], vparts[:, u, 1, :], ALU.subtract)\
                        .then_inc(S["rest2_ready"], 1)
                elif kind == "G":
                    pool.wait_ge(S["absmax"], 1)
                    pool.partition_all_reduce(gm[:, 1, :], gm[:, 0, :], P, RMAX).then_inc(S["allmax"], 1)
                elif kind == "scan":
                    s = item[1]
                    q, j = SCANS[s]
                    pool.wait_ge(S["state_ready"], s + 1)
                    if s >= PRODS:
                        pool.wait_ge(S["sum_done"], s - PRODS + 1)
                    if j == 0:
                        pool.wait_ge(S["job_used"], used_jobs(unit_no(R, *PASSES[q])))
                    pool.tensor_tensor(prod[:, s % PRODS, :], state[:, s % STATES, :], unit(R, q), ALU.mult)\
                        .then_inc(S["prod_ready"], 1)
                elif kind == "fin":
                    q = item[1]
                    pool.wait_ge(S["half_read"], q + 1)
                    pool.wait_ge(S["job_used"], used_jobs(unit_no(G, *PASSES[q])))
                    pool.tensor_tensor(og_cols(q), og_cols(q), unit(G, q), ALU.mult).then_inc(S["og_ready"], 1)
                elif kind == "piece":
                    d = item[1]
                    w, e, f = PIECES[d]
                    pool.wait_ge(S["scale_ready"], w + 1)
                    pool.wait_ge(S["bits_ready"], d + 1)
                    if d >= 2:
                        pool.wait_ge(S["lo_ready"], d - 1)
                    pool.tensor_tensor(full[:, d % 2, :], bits[:, 1 + d % 2, :].bitcast(F16),
                                       scales[:, w, PC * f:PC * f + PC], ALU.mult).then_inc(S["full_ready"], 1)
                elif kind == "low" and item[1] >= POOL_LOW:
                    low_part(pool, item[1])
                elif kind == "aff0":
                    pool.wait_ge(loaded["xtok"], 16)
                    pool.wait_ge(loaded["ln"], 16)
                    xp = xtok[:, pair_of(item), :]
                    pool.tensor_tensor(xp, xp, ln[:, 1:2, :].broadcast_to([P, 2, C]), ALU.add).then_inc(S["xlb_ready"], 1)
                elif kind == "aff":
                    g, pair = item[1:]
                    zp = ztmp[:, pair_of(item), :]
                    pool.wait_ge(S["normal_ready"], normals_before(0, g) - 2 * (1 - pair))
                    step(pool.tensor_tensor(zp, zp, ln[:, 0:1, :].broadcast_to([P, 2, C]), ALU.mult))
                    pool.wait_ge(pool_steps, steps[0])
                    pool.wait_ge(S["xlb_ready"], 2 * g + pair + 1)
                    pool.tensor_tensor(zp, zp, xtok[:, pair_of(item), :], ALU.add).then_inc(S["z_ready"], 1)

        @block.tensor
        def _(pe):
            for item in plan_of("tensor"):
                kind = item[0]
                if kind in ("proj", "qk", "energy", "attT"):
                    job = JOBS.index(item)
                    ps = job_ps[job % 2]
                    if job >= 2:
                        pe.wait_ge(S["job_used"], job - 1)
                if kind == "proj":
                    m, g, h = UNITS[item[1]]
                    i = MIXES.index((m, g))
                    pe.wait_ge(loaded[vp_weight(m)], 16)
                    for k in range(2):
                        pe.wait_ge(S["mix_ready"], 2 * i + k + 1)
                        mm = pe.matmul(ps, wproj[:, m, k, P * h:P * h + P], mix[:, i % 4, k, :], start=(k == 0), stop=(k == 1))
                    mm.then_inc(S["job_done"], 1)
                elif kind == "qk":
                    m, g = item[1] // 2, item[1] % 2
                    pe.wait_ge(loaded["ctx"], 16)
                    pe.wait_ge(loaded["wqk"], 16)
                    pe.matmul(ps, wqk[:, m, :], ctxT[:, TB * g:TB * g + TB], start=True, stop=True).then_inc(S["job_done"], 1)
                elif kind == "energy":
                    i = item[1]
                    pe.wait_ge(S["job_used"], JOBS.index(("qk", 3)) + 1)
                    for n in (2 * i, 2 * i + 1):
                        mm = pe.matmul(ps[:, (n % 2) * T:(n % 2) * T + T], queryT[:, P * n:P * n + P],
                                       keyT[:, T * (n // 2):T * (n // 2) + T], start=True, stop=True)
                    mm.then_inc(S["job_done"], 1)
                elif kind == "attT":
                    i = item[1]
                    pe.wait_ge(S["att_ready"], 2 * i + 2)
                    for n in range(2):
                        for k in range(2):
                            mm = pe.transpose(ps[:, (2 * n + k) * P:(2 * n + k + 1) * P], att[:, 2 * i + n, P * k:P * k + P],
                                              ident)
                    mm.then_inc(S["job_done"], 1)
                elif kind == "spread":
                    i = item[1]
                    q, j = SPREADS[i]
                    g, h = PASSES[q]
                    if i >= 2:
                        pe.wait_ge(S["spread_used"], i - 1)
                    if j is None:
                        pe.wait_ge(loaded["const"], 16)
                        pe.wait_ge(S["diag_ready"], q + 1)
                        mm = pe.matmul(spread_ps[i % 2], head_sum, diag, start=True, stop=True)
                    elif q == 0 and j < FIRST:
                        pe.wait_ge(S["spread_w_ready"], FIRST)
                        pe.wait_ge(S["job_used"], used_jobs(0))
                        mm = pe.matmul(spread_ps[i % 2], first_w[:, j, :], unit(V, q), start=True, stop=True)
                    else:
                        pe.wait_ge(S["spread_w_ready"], FIRST + 4)
                        if j % 4 == 0:
                            pe.wait_ge(stacked[q][j // 4], 48)
                        mm = pe.matmul(spread_ps[i % 2], spread_w[:, j % 4, :], vstack[h][:, j // 4, TB * g:TB * g + TB],
                                       start=True, stop=True)
                    mm.then_inc(S["spread_done"], 1)
                elif kind == "sum":
                    s = item[1]
                    q, j = SCANS[s]
                    pe.wait_ge(loaded["const"], 16)
                    pe.wait_ge(S["prod_ready"], s + 1)
                    if j == 0 and q >= 2:
                        pe.wait_ge(S["half_read"], q - 1)
                    pe.matmul(sum_ps[q % 2], head_pick[:, 8 * (15 - j):8 * (15 - j) + P], prod[:, s % PRODS, :],
                              start=(j == 0), stop=(j == D - 1)).then_inc(S["sum_done"], 1)
                elif kind == "y":
                    g = item[1]
                    pe.wait_ge(loaded["wo"], 16)
                    pe.wait_ge(S["og_ready"], 2 * g + 2)
                    if g == 0:
                        pe.wait_ge(S["job_used"], len(JOBS))
                    for n in tiles_of(g):
                        for k in range(2):
                            mm = pe.matmul(ps_tile(g, n), og[:, k, P * n:P * n + P], wo[:, k, :], start=(k == 0), stop=(k == 1))
                    mm.then_inc(S["y_done"], 1)
                elif kind == "x1T":
                    g = item[1]
                    pe.wait_ge(S["normal_ready"], normals_before(1, g))
                    for k in range(2):
                        for n in tiles_of(g):
                            at = k * TB + (n % GT) * P
                            mm = pe.transpose(psA[g][:, at:at + P], x1[:, n, P * k:P * k + P], ident)
                    mm.then_inc(S["x1T_done"], 1)
                elif kind == "xm":
                    g = item[1]
                    pe.wait_ge(S["x1T_ready"], g + 1)
                    for n in tiles_of(g):
                        b = n * P // T
                        for k in range(2):
                            mm = pe.matmul(ps_tile(g, n), x1T[:, k, (n % GT) * P:(n % GT) * P + P],
                                           attT[:, k, 2 * b:2 * b + 2, :], start=(k == 0), stop=(k == 1))
                    mm.then_inc(S["xm_done"], 1)
                elif kind == "x2T":
                    g = item[1]
                    pe.wait_ge(S["normal_ready"], normals_before(2, g))
                    for k in range(2):
                        for n in tiles_of(g):
                            at = k * TB + (n % GT) * P
                            mm = pe.transpose(psA[g][:, at:at + P], x2[:, n, k:C:2], ident)
                    mm.then_inc(S["x2T_done"], 1)
                elif kind == "hidden":
                    g, n = item[1:]
                    s = NT * g + n
                    if n == 0:
                        pe.wait_ge(S["x2lo_ready"], g + 1)
                    if g == 0:
                        pe.wait_ge(S["lo_ready"], pieces_for(n * P // PC))
                    if s == 1:
                        pe.wait_ge(S["spread_used"], len(SPREADS))
                    if s == 2:
                        pe.wait_ge(S["half_read"], len(PASSES))
                    for w, done, used in ((0, "gate_done", "gelu_done"), (1, "up_done", "inter_ready")):
                        if s >= 3:
                            pe.wait_ge(S[used], s - 2)
                        passes = [(k, a, b) for k in range(2) for a, b in ((0, 0), (0, 1), (1, 0))]
                        for i, (k, a, b) in enumerate(passes):
                            mm = pe.matmul(hidden_ps(s)[w], w16[:, w, k, a, n * P:n * P + P], x2T16[:, b, g, k, :],
                                           start=(i == 0), stop=(i == 5))
                        mm.then_inc(S[done], 1)
                elif kind == "down":
                    g = item[1]
                    pe.wait_ge(S["lo_ready"], len(PIECES))
                    if g:
                        pe.wait_ge(S["var_ready"], norm_no(3, 0) + 1)
                    else:
                        pe.wait_ge(S["gelu_done"], NT)
                    for n in tiles_of(g):
                        at = (n % GT) * P
                        passes = [(m, a, b) for m in range(NT) for a, b in ((0, 0), (0, 1), (1, 0))]
                        for i, (m, a, b) in enumerate(passes):
                            if n % GT == 0 and i % 3 == 0:
                                pe.wait_ge(S["ilo_ready"], NT * g + m + 1)
                            mm = pe.matmul(down_tile(g, n), inter[g][:, a, m, at:at + P],
                                           w16[:, 2, m % 2, b, (m // 2) * C:(m // 2) * C + C],
                                           start=(i == 0), stop=(i == len(passes) - 1))
                        mm.then_inc(S["down_done"], 1)

        @block.vector
        def _(dve):
            steps = [0]

            def step(ins):
                steps[0] += 1
                ins.then_inc(vec, 1)

            def own():
                dve.wait_ge(vec, steps[0])

            def stats(i, g, tiles, src):
                for n in tiles:
                    step(dve.bn_stats(lnst[:, n % GT, :], src(n)))
                own()
                for n in tiles:
                    ins = dve.bn_aggr(mv[:, i, n, :], lnst[:, n % GT, :])
                    if n != tiles[-1]:
                        step(ins)
                ins.then_inc(S["var_ready"], 1)

            def rows(i, g, tiles):
                a, b = tiles[0], tiles[-1] + 1
                dve.wait_ge(S["sqrt_done"], norm_no(i, g, tiles) + 1)
                step(dve.reciprocal(rstd[:, i, a:b], rstd[:, i, a:b]))
                own()
                dve.wait_ge(S["var_ready"], norm_no(i, g, tiles) + 1)
                dve.scalar_tensor_tensor(out=shift[:, i, a:b], in0=mv[:, i, a:b, 0], scalar=-1.0, in1=rstd[:, i, a:b],
                                         op0=ALU.mult, op1=ALU.mult).then_inc(S["rows_ready"], 1)

            kvb = [kv[:, s, :].rearrange("p (b t) -> p b t", t=T) for s in range(2)]
            step(dve.memset(keep[:, :], 1.0))
            own()
            step(dve.memset(keep[:, 0:TB:T], 0.0))
            step(dve.memset(eps[:, :], EPS))
            for s in range(2):
                step(dve.memset(kvb[s][:, :, 0:1], 0.0))

            for item in plan_of("vector"):
                kind = item[0]
                if kind == "xx":
                    g = item[1]
                    for h in range(2):
                        dve.wait_ge(loaded[f"x{g}_half{h}"], 16)
                        xb = xT[:, h, TB * g:TB * g + TB].rearrange("p (b t) -> p b t", t=T)
                        xxb = xx[:, h, TB * g:TB * g + TB].rearrange("p (b t) -> p b t", t=T)
                        step(dve.tensor_tensor(xxb[:, :, 1:T], xb[:, :, 0:T - 1], xb[:, :, 1:T], ALU.subtract))
                        step(dve.tensor_tensor(xxb[:, :, 0:1], xb[:, :, 1:2], xb[:, :, 0:1], ALU.subtract))
                    xx_at = steps[0]
                elif kind == "mix":
                    i = item[1]
                    m, g = MIXES[i]
                    dve.wait_ge(vec, xx_at)
                    if i == 0:
                        dve.wait_ge(loaded["cvec"], 16)
                    if i >= 4:
                        dve.wait_ge(S["job_done"], used_jobs(unit_no(m, 0, 1)))
                    for h in range(2):
                        dve.scalar_tensor_tensor(out=mix[:, i % 4, h, :], in0=xx[:, h, TB * g:TB * g + TB],
                                                 scalar=cvec[:, h, m:m + 1], in1=xT[:, h, TB * g:TB * g + TB],
                                                 op0=ALU.mult, op1=ALU.add).then_inc(S["mix_ready"], 1)
                elif kind == "first_w":
                    dve.wait_ge(loaded["spreads"], 16)
                    for j in range(FIRST):
                        dve.tensor_scalar(first_w[:, j, :], head_spread, lane[:, 4 + j:5 + j], None, ALU.mult)\
                           .then_inc(S["spread_w_ready"], 1)
                elif kind == "spread_w":
                    for j in range(4):
                        dve.tensor_scalar(spread_w[:, j, :], head_spread[0:96, :], lane[0:96, j:j + 1], None, ALU.mult)\
                           .then_inc(S["spread_w_ready"], 1)
                elif kind == "diag":
                    q = item[1]
                    g, h = PASSES[q]
                    dve.wait_ge(S["job_used"], used_jobs(unit_no(R, g, h)))
                    if q:
                        dve.wait_ge(S["spread_done"], SPREADS.index((q - 1, None)) + 1)
                    dve.scalar_tensor_tensor(out=diag, in0=unit(K, q), scalar=cvec[:, h, 5:6], in1=unit(R, q),
                                             op0=ALU.mult, op1=ALU.mult).then_inc(S["diag_ready"], 1)
                elif kind == "use":
                    i = item[1]
                    q, j = SPREADS[i]
                    dve.wait_ge(S["spread_done"], i + 1)
                    if j is None:
                        dve.wait_ge(S["rest2_ready"], q + 1)
                        dve.tensor_tensor(og_cols(q), spread_ps[i % 2], unit(V, q), ALU.mult).then_inc(S["spread_used"], 1)
                    else:
                        s = SCANS.index((q, j))
                        if s >= 2:
                            dve.wait_ge(S["state_ready"], s - 1)
                        if j == 0:
                            dve.wait_ge(S["job_used"], used_jobs(unit_no(K, *PASSES[q])))
                        vb = spread_ps[i % 2].rearrange("p (b t) -> p b t", t=T)
                        kb = unit(K, q).rearrange("p (b t) -> p b t", t=T)
                        dve.tensor_tensor(kvb[s % 2][:, :, 1:T], vb[:, :, 0:T - 1], kb[:, :, 0:T - 1], ALU.mult)\
                           .then_inc(S["spread_used"], 1)
                elif kind == "scan":
                    s = item[1]
                    q, j = SCANS[s]
                    h = PASSES[q][1]
                    dve.wait_ge(S["spread_used"], SPREADS.index((q, j)) + 1)
                    if s == 0:
                        dve.wait_ge(S["decay_set"], 2)
                        own()
                    if s >= STATES:
                        dve.wait_ge(S["prod_ready"], s - STATES + 1)
                    dve.tensor_tensor_scan(state[:, s % STATES, :], decay_ps[:, TB * h:TB * h + TB], kv[:, s % 2, :], 0.0,
                                           ALU.mult, ALU.add).then_inc(S["state_ready"], 1)
                elif kind == "flat":
                    dve.wait_ge(loaded["flat"], 16)
                    dve.tensor_reduce(gm[:, 0, :], flat, AX.X, ALU.max, apply_absolute_value=True)\
                       .then_inc(S["absmax"], 1)
                elif kind == "fin":
                    q = item[1]
                    dve.wait_ge(S["sum_done"], D * (q + 1))
                    dve.wait_ge(S["spread_used"], SPREADS.index((q, None)) + 1)
                    dve.tensor_tensor(og_cols(q), sum_ps[q % 2], og_cols(q), ALU.add).then_inc(S["half_read"], 1)
                elif kind == "G":
                    dve.wait_ge(S["allmax"], 1)
                    step(dve.tensor_scalar(gm[:, 1, :], gm[:, 1, :], 2.0 ** -60, None, ALU.max))
                    own()
                    step(dve.tensor_scalar(gm[:, 2, :].bitcast(I32), gm[:, 1, :].bitcast(I32), 0x7F800000, None,
                                           ALU.bitwise_and))
                    own()
                    step(dve.reciprocal(gm[:, 5, :], gm[:, 2, :]))
                    own()
                    dve.tensor_scalar(gm[:, 3, :], gm[:, 5, :], W_UP * CODE_UP, None, ALU.mult).then_inc(S["g_ready"], 1)
                    step(dve.tensor_scalar(gm[:, 4, 0:1], gm[:, 2, 0:1], 1.0 / (X_UP * W_UP), None, ALU.mult))
                    step(dve.tensor_scalar(gm[:, 4, 1:2], gm[:, 5, 0:1], I_DOWN / (X_UP * W_UP), None, ALU.mult))
                    step(dve.tensor_tensor(gm[:, 6, 0:1], gm[:, 2, 0:1], gm[:, 2, 1:2], ALU.mult))
                    own()
                    step(dve.tensor_scalar(gm[:, 4, 2:3], gm[:, 6, 0:1], gm[:, 2, 2:3], 1.0 / (I_DOWN * W_UP),
                                           ALU.mult, ALU.mult))
                elif kind == "piece":
                    d = item[1]
                    w, e, f = PIECES[d]
                    dve.wait_ge(S["codes_ready"], w + 1)
                    if d == 0:
                        dve.wait_ge(S["mix_ready"], 2 * len(MIXES))
                    else:
                        dve.wait_ge(S["bits_ready"], d)
                    if d >= 2:
                        dve.wait_ge(S["full_ready"], d - 1)
                    src = p16[:, w, PC * f:PC * f + PC].bitcast(U32)
                    magnitude, code = bits[:, 0, :].bitcast(U32), bits[:, 1 + d % 2, :].bitcast(U32)
                    step(dve.tensor_scalar(magnitude, src, 9 - 4 * e, 0x0E000E00, ALU.logical_shift_left, ALU.bitwise_and))
                    step(dve.tensor_scalar(code, src, 12 - 4 * e, 0x80008000, ALU.logical_shift_left, ALU.bitwise_and))
                    own()
                    dve.tensor_tensor(code, code, magnitude, ALU.bitwise_or).then_inc(S["bits_ready"], 1)
                elif kind == "low" and item[1] < POOL_LOW:
                    low_part(dve, item[1])
                elif kind == "energy":
                    i = item[1]
                    job = JOBS.index(item)
                    dve.wait_ge(S["job_done"], job + 1)
                    dve.tensor_reduce(smax[:, 0, 2 * i:2 * i + 2], job_ps[job % 2].rearrange("p (n k) -> p n k", n=2),
                                      AX.X, ALU.max, negate=True).then_inc(S["negmax_ready"], 1)
                elif kind == "rowsum":
                    dve.wait_ge(S["job_used"], JOBS.index(("energy", 3)) + 1)
                    dve.reciprocal(smax[:, 2, :], smax[:, 1, :]).then_inc(S["recip_ready"], 1)
                elif kind == "stat0":
                    g = item[1]
                    dve.wait_ge(S["y_done"], g + 1)
                    stats(0, g, tiles_of(g), lambda n: ps_tile(g, n))
                elif kind == "stat1":
                    g = item[1]
                    dve.wait_ge(S["z_ready"], 2 * g + 2)
                    stats(1, g, tiles_of(g), lambda n: ztmp[:, n, :])
                elif kind in ("rows0", "rows1", "rows2"):
                    rows(int(kind[-1]), item[1], tiles_of(item[1]))
                elif kind == "stat2":
                    g = item[1]
                    dve.wait_ge(S["xm_done"], g + 1)
                    zg = ztmp[:, GT * g:GT * g + GT, :]
                    step(dve.tensor_tensor(zg, psA[g][:, :].rearrange("p (n c) -> p n c", n=GT),
                                           x1[:, GT * g:GT * g + GT, :], ALU.add))
                    own()
                    stats(2, g, tiles_of(g), lambda n: ztmp[:, n, :])
                elif kind == "x2lo":
                    g = item[1]
                    dve.wait_ge(S["x2hi_ready"], g + 1)
                    dve.scalar_tensor_tensor(out=x2T16[:, 1, g, :, :],
                                             in0=psA[g][:, :].rearrange("p (k t) -> p k t", k=2), scalar=X_UP,
                                             in1=x2T16[:, 0, g, :, :], op0=ALU.mult, op1=ALU.subtract)\
                       .then_inc(S["x2lo_ready"], 1)
                elif kind == "ffn":
                    g, n = item[1:]
                    s = NT * g + n
                    dve.wait_ge(S["gelu_done"], s + 1)
                    dve.wait_ge(S["up_done"], s + 1)
                    if s == 0:
                        dve.wait_ge(S["prod_ready"], len(SCANS))
                    if s >= 2:
                        dve.wait_ge(S["ilo_ready"], s - 1)
                    dve.scalar_tensor_tensor(out=inter32[:, s % 2, :], in0=hidden_ps(s)[1], scalar=gm[:, 4, 1:2],
                                             in1=gelu[:, s % 2, :], op0=ALU.mult, op1=ALU.mult).then_inc(S["inter_ready"], 1)
                elif kind == "split":
                    g, n = item[1:]
                    s = NT * g + n
                    if s == 0:
                        dve.wait_ge(S["og_ready"], len(PASSES))
                    if s == NT // 2:
                        dve.wait_ge(S["y_done"], 2)
                    dve.wait_ge(S["ihi_ready"], s + 1)
                    dve.tensor_tensor(inter[g][:, 1, n, :], inter32[:, s % 2, :], inter[g][:, 0, n, :], ALU.subtract)\
                       .then_inc(S["ilo_ready"], 1)
                elif kind == "out":
                    g = item[1]
                    done = GT * g
                    for tiles in out_chunks(g):
                        a, b = tiles[0], tiles[-1] + 1
                        done += len(tiles)
                        dve.wait_ge(S["down_done"], done)
                        dve.wait_ge(S["normal_ready"], normals_before(2, g))
                        step(dve.scalar_tensor_tensor(
                            out=ff[:, a:b, :].rearrange("p n c -> p (n c)"),
                            in0=psA[0][:, :] if g == 0 else down_tile(g, a), scalar=gm[:, 4, 2:3],
                            in1=x2[:, a:b, :].rearrange("p n c -> p (n c)"), op0=ALU.mult, op1=ALU.add))
                        own()
                        stats(3, g, tiles, lambda n: ff[:, n, :])
                        rows(3, g, tiles)


def kernel(**inputs):
    import numpy as np
    import concourse.bacc as bacc
    from concourse.bass_utils import run_bass_kernel_spmd

    a = {k: np.asarray(v) for k, v in inputs.items()}
    n, c = N, C

    def hidden_order(w):
        return w.reshape(w.shape[0], 8, P, 2).transpose(0, 1, 3, 2).reshape(w.shape[0], MLP)

    def dim_major(w):
        return w.reshape(2, HPH, D, -1).transpose(0, 2, 1, 3).reshape(c, -1)

    x = a["x"].reshape(n, c)
    gate, up, down = (a[f"L0_ffn_{m}_W_packed"] for m in ("gate", "up", "down"))
    sg, su, sd = (a[f"L0_ffn_{m}_scales"] for m in ("gate", "up", "down"))
    lanes = np.arange(P)
    to_sum = (lanes[:, None] // D == lanes[None, :] % HPH).astype(np.float32)
    pick = np.zeros((P, 248), np.float32)
    pick[lanes, 120 + lanes // D] = 1.0
    consts = np.concatenate([np.eye(P, dtype=np.float32), to_sum, pick, to_sum.T,
                             (lanes[:, None] // HPH % 4 == np.arange(4)[None, :]).astype(np.float32),
                             (lanes[:, None] // HPH == np.arange(FIRST)[None, :]).astype(np.float32)], axis=1)
    data = {
        "x_chan": x.T,
        "x_tok": x,
        "ctx_chan": a["ctx_1024"].reshape(n, P).T,
        "w_chan": np.stack([dim_major(a["L0_attn_Wv"]).T, a["L0_attn_Wk"].T, a["L0_attn_Wr"].T,
                            dim_major(a["L0_attn_Wg"]).T, dim_major(a["L0_attn_Wo"].T)]),
        "chan_vecs": np.stack([a["L0_attn_tm_" + m] for m in "vkrg"] + [a["L0_attn_time_decay"].reshape(c),
                              a["L0_attn_time_first"].reshape(c)], axis=1),
        "ln_vecs": np.stack([a["L0_attn_ln_w"], a["L0_attn_ln_b"]]),
        "xq_chan": np.stack([a["L0_xattn_Wq"].T, a["L0_xattn_Wk"].T]),
        "xq_bias": np.stack([a["L0_xattn_bq"], a["L0_xattn_bk"]], axis=1),
        "packed": np.stack([hidden_order(gate.T), hidden_order(up.T),
                            down.T.reshape(8, P, c).transpose(1, 0, 2).reshape(P, MLP)]),
        "scale_rows_in": np.stack([hidden_order(sg.T), hidden_order(su.T)]),
        "scale_rows_out": sd.T.reshape(8, 8, c),
        "scale_flat": np.stack([sg.reshape(-1), su.reshape(-1), sd.reshape(-1)]),
        "consts": consts,
    }
    nc = bacc.Bacc("TRN2", target_bir_lowering=False, num_devices=1)
    arrays, args = {}, []
    for name, value in data.items():
        value = np.ascontiguousarray(value)
        arrays[name] = value
        args.append(nc.dram_tensor(name, value.shape, mybir.dt.from_np(value.dtype), kind="ExternalInput").ap())
    args.append(nc.dram_tensor("out", (n, c), F32, kind="ExternalOutput").ap())
    decoder_layer(nc, *args)
    result = run_bass_kernel_spmd(nc, [arrays], core_ids=[0])
    return result.results[0]["out"].reshape(B, T, C)
```
